# Optimizing a Trainium2 kernel written in Bass

```python
import numpy as np
import jax
import jax.numpy as jnp

def _softmax(x, axis=-1):
    return jax.nn.softmax(x, axis=axis)

def _gelu(x):
    return jax.nn.gelu(x, approximate=True)

def _silu(x):
    return jax.nn.silu(x)

def _sigmoid(x):
    return jax.nn.sigmoid(x)

def _layernorm(x, axis=-1, eps=1e-05):
    m = jnp.mean(x, axis=axis, keepdims=True)
    v = jnp.var(x, axis=axis, keepdims=True)
    return (x - m) / jnp.sqrt(v + eps)

def _scatter_add(tgt, idx, src, axis=0):
    return tgt.at[idx].add(src)

def _segment_sum(src, seg, n):
    return jax.ops.segment_sum(src, seg, n)
kernel_name = 'mk_decoder_preln_d1_seqx_r8_6cd3f8'

def setup_inputs(seed: int=0):
    np.random.seed(seed)
    _w = jnp.asarray

    def _rec_inputs():
        import jax
        import jax.numpy as jnp
        _rk = jax.random.key(seed)
        x = -0.0003929 + 0.9999 * jax.random.normal(jax.random.fold_in(_rk, 1), (8, 128, 256), jnp.float32)
        _lenS = 128 - jax.random.randint(jax.random.fold_in(_rk, 7), (8,), 0, max(1, 128 // 4) + 1, jnp.int32)
        _lenS2 = 128 - jax.random.randint(jax.random.fold_in(_rk, 8), (8,), 0, max(1, 128 // 4) + 1, jnp.int32)
        _ctx_2048P = jax.random.normal(jax.random.fold_in(_rk, 11), (8, 16, 256), jnp.float32)
        _ctx_2048c = jax.random.dirichlet(jax.random.fold_in(_rk, 511), 0.3 * jnp.ones((16,), jnp.float32), (8, 128))
        _ctx_2048t = jnp.einsum('bsk,bkd->bsd', _ctx_2048c, _ctx_2048P)
        _ctx_2048t = _ctx_2048t * jax.lax.rsqrt(jnp.mean(jnp.square(_ctx_2048t)) + 1e-12) * 0.953939
        ctx_2048 = 2.81802e-05 + 1.00001 * (_ctx_2048t + 0.3 * jax.random.normal(jax.random.fold_in(_rk, 611), (8, 128, 256), jnp.float32))
        return (x, ctx_2048)
    x, ctx_2048 = _rec_inputs()

    def _L0_attn_setup():
        import jax, jax.numpy as jnp
        import numpy as np
        N_EMBED = 256
        N_HEAD = 16
        N_GROUP = 4
        D_HEAD = N_EMBED // N_HEAD
        GROUP_SIZE = N_HEAD // N_GROUP
        SLIDING_WINDOW = 64
        ATTENTION_SINK = 4
        POS = 0
        ROPE_BASE = 10000.0

        def _rope(x, pos):
            B, T, H, d = x.shape
            half = d // 2
            inv_freq = 1.0 / ROPE_BASE ** (jnp.arange(half, dtype=jnp.float32) * 2.0 / d)
            t = jnp.arange(T, dtype=jnp.float32) + pos
            ang = t[:, None] * inv_freq[None, :]
            cos = jnp.cos(ang)[None, :, None, :].astype(x.dtype)
            sin = jnp.sin(ang)[None, :, None, :].astype(x.dtype)
            x1, x2 = (x[..., :half], x[..., half:])
            return jnp.concatenate([x1 * cos - x2 * sin, x1 * sin + x2 * cos], axis=-1)

        def _sliding_mask(q_len, kv_len):
            i = jnp.arange(q_len)[:, None]
            j = jnp.arange(kv_len)[None, :]
            causal = i >= j
            sink = j < ATTENTION_SINK
            local = j >= i - SLIDING_WINDOW
            return causal & (local | sink)
        key = jax.random.key(seed)
        ks = jax.random.split(key, 9)
        s_in = 1.0 / np.sqrt(N_EMBED)
        x = jax.random.normal(ks[0], (2, 256, N_EMBED), dtype=jnp.float32)
        Wq = jax.random.uniform(ks[1], (N_EMBED, N_HEAD * D_HEAD), jnp.float32, -s_in, s_in)
        bq = jax.random.uniform(ks[2], (N_HEAD * D_HEAD,), jnp.float32, -s_in, s_in)
        Wk = jax.random.uniform(ks[3], (N_EMBED, N_GROUP * D_HEAD), jnp.float32, -s_in, s_in)
        bk = jax.random.uniform(ks[4], (N_GROUP * D_HEAD,), jnp.float32, -s_in, s_in)
        Wv = jax.random.uniform(ks[5], (N_EMBED, N_GROUP * D_HEAD), jnp.float32, -s_in, s_in)
        bv = jax.random.uniform(ks[6], (N_GROUP * D_HEAD,), jnp.float32, -s_in, s_in)
        Wo = jax.random.uniform(ks[7], (N_EMBED, N_EMBED), jnp.float32, -s_in, s_in)
        bo = jax.random.uniform(ks[8], (N_EMBED,), jnp.float32, -s_in, s_in)
        return {'x': x, 'Wq': Wq, 'bq': bq, 'Wk': Wk, 'bk': bk, 'Wv': Wv, 'bv': bv, 'Wo': Wo, 'bo': bo}
    _L0_attn_all = _L0_attn_setup()
    _L0_attn_in = {k: v for k, v in _L0_attn_all.items() if k in ('Wq', 'bq', 'Wk', 'bk', 'Wv', 'bv', 'Wo', 'bo')}
    del _L0_attn_all

    def _L0_xattn_setup():
        import jax, jax.numpy as jnp
        import numpy as np
        HIDDEN = 256
        NUM_HEADS = 16
        HEAD_DIM = HIDDEN // NUM_HEADS
        CHUNK = 128
        SCALE = HEAD_DIM ** (-0.5)

        def _chunked_causal_attention(q, k, v):
            B, H, S, D = q.shape
            n_chunks = S // CHUNK
            kc = k.reshape(B, H, n_chunks, CHUNK, D).transpose(2, 0, 1, 3, 4)
            vc = v.reshape(B, H, n_chunks, CHUNK, D).transpose(2, 0, 1, 3, 4)
            j0s = jnp.arange(n_chunks) * CHUNK
            q_idx = jnp.arange(S)[:, None]
            k_off = jnp.arange(CHUNK)[None, :]
            out0 = jnp.zeros_like(q)
            m0 = jnp.full((B, H, S, 1), -jnp.inf, dtype=q.dtype)
            s0 = jnp.zeros((B, H, S, 1), dtype=q.dtype)

            def step(carry, inputs):
                out, m, s = carry
                kj, vj, j0 = inputs
                scores = jnp.einsum('bhqd,bhkd->bhqk', q, kj) * SCALE
                causal = j0 + k_off > q_idx
                scores = jnp.where(causal[None, None], -jnp.inf, scores)
                chunk_max = scores.max(axis=-1, keepdims=True)
                new_m = jnp.maximum(m, chunk_max)
                exp_old = jnp.exp(m - new_m)
                exp_c = jnp.exp(scores - new_m)
                new_s = s * exp_old + exp_c.sum(axis=-1, keepdims=True)
                out = out * (s / new_s) * exp_old + jnp.einsum('bhqk,bhkd->bhqd', exp_c / new_s, vj)
                return ((out, new_m, new_s), None)
            (out, _, _), _ = jax.lax.scan(step, (out0, m0, s0), (kc, vc, j0s))
            return out
        key = jax.random.key(seed)
        kq, kk, kv = jax.random.split(key, 3)
        B, S = (2, 512)
        return {'query': jax.random.normal(kq, (B, S, HIDDEN), dtype=jnp.float32), 'key': jax.random.normal(kk, (B, S, HIDDEN), dtype=jnp.float32), 'value': jax.random.normal(kv, (B, S, HIDDEN), dtype=jnp.float32)}
    _L0_xattn_all = _L0_xattn_setup()
    _L0_xattn_in = {k: v for k, v in _L0_xattn_all.items() if k in ()}
    del _L0_xattn_all

    def _L0_ffn_setup():
        import jax, jax.numpy as jnp
        import numpy as np
        TOP_K = 4

        def _silu_and_mul(gu):
            g, u = jnp.split(gu, 2, axis=-1)
            return jax.nn.silu(g) * u
        key = jax.random.key(seed)
        ks = jax.random.split(key, 7)
        H, E, I, Is = (256, 16, 176, 704)
        s = 0.02
        return {'hidden_states': jax.random.normal(ks[0], (4, 128, H), dtype=jnp.float32), 'gate_w': jax.random.normal(ks[1], (E, H), dtype=jnp.float32) * s, 'sgate_w': jax.random.normal(ks[2], (1, H), dtype=jnp.float32) * s, 'w13': jax.random.normal(ks[3], (E, 2 * I, H), dtype=jnp.float32) * s, 'w2': jax.random.normal(ks[4], (E, H, I), dtype=jnp.float32) * s, 'shared_gate_up_w': jax.random.normal(ks[5], (2 * Is, H), dtype=jnp.float32) * s, 'shared_down_w': jax.random.normal(ks[6], (H, Is), dtype=jnp.float32) * s}
    _L0_ffn_all = _L0_ffn_setup()
    _L0_ffn_in = {k: v for k, v in _L0_ffn_all.items() if k in ('gate_w', 'sgate_w', 'w13', 'w2', 'shared_gate_up_w', 'shared_down_w')}
    del _L0_ffn_all
    return {'x': x, 'ctx_2048': ctx_2048, 'L0_attn_Wq': _L0_attn_in['Wq'], 'L0_attn_bq': _L0_attn_in['bq'], 'L0_attn_Wk': _L0_attn_in['Wk'], 'L0_attn_bk': _L0_attn_in['bk'], 'L0_attn_Wv': _L0_attn_in['Wv'], 'L0_attn_bv': _L0_attn_in['bv'], 'L0_attn_Wo': _L0_attn_in['Wo'], 'L0_attn_bo': _L0_attn_in['bo'], 'L0_ffn_gate_w': _L0_ffn_in['gate_w'], 'L0_ffn_sgate_w': _L0_ffn_in['sgate_w'], 'L0_ffn_w13': _L0_ffn_in['w13'], 'L0_ffn_w2': _L0_ffn_in['w2'], 'L0_ffn_shared_gate_up_w': _L0_ffn_in['shared_gate_up_w'], 'L0_ffn_shared_down_w': _L0_ffn_in['shared_down_w']}

def reference(x, ctx_2048, L0_attn_Wq, L0_attn_bq, L0_attn_Wk, L0_attn_bk, L0_attn_Wv, L0_attn_bv, L0_attn_Wo, L0_attn_bo, L0_ffn_gate_w, L0_ffn_sgate_w, L0_ffn_w13, L0_ffn_w2, L0_ffn_shared_gate_up_w, L0_ffn_shared_down_w):
    import jax
    import jax.numpy as jnp

    def _L0_attn_ref(x, Wq, bq, Wk, bk, Wv, bv, Wo, bo):
        import jax, jax.numpy as jnp
        import numpy as np
        N_EMBED = 256
        N_HEAD = 16
        N_GROUP = 4
        D_HEAD = N_EMBED // N_HEAD
        GROUP_SIZE = N_HEAD // N_GROUP
        SLIDING_WINDOW = 64
        ATTENTION_SINK = 4
        POS = 0
        ROPE_BASE = 10000.0

        def _rope(x, pos):
            B, T, H, d = x.shape
            half = d // 2
            inv_freq = 1.0 / ROPE_BASE ** (jnp.arange(half, dtype=jnp.float32) * 2.0 / d)
            t = jnp.arange(T, dtype=jnp.float32) + pos
            ang = t[:, None] * inv_freq[None, :]
            cos = jnp.cos(ang)[None, :, None, :].astype(x.dtype)
            sin = jnp.sin(ang)[None, :, None, :].astype(x.dtype)
            x1, x2 = (x[..., :half], x[..., half:])
            return jnp.concatenate([x1 * cos - x2 * sin, x1 * sin + x2 * cos], axis=-1)

        def _sliding_mask(q_len, kv_len):
            i = jnp.arange(q_len)[:, None]
            j = jnp.arange(kv_len)[None, :]
            causal = i >= j
            sink = j < ATTENTION_SINK
            local = j >= i - SLIDING_WINDOW
            return causal & (local | sink)
        B, T, C = x.shape
        scale = D_HEAD ** (-0.5)
        Q = (x @ Wq + bq).reshape(B, T, N_HEAD, D_HEAD)
        K = (x @ Wk + bk).reshape(B, T, N_GROUP, D_HEAD)
        V = (x @ Wv + bv).reshape(B, T, N_GROUP, D_HEAD)
        Q = _rope(Q, POS)
        K = _rope(K, POS)
        Q = Q.transpose(0, 2, 1, 3).reshape(B, N_GROUP, GROUP_SIZE, T, D_HEAD)
        K = K.transpose(0, 2, 1, 3)
        V = V.transpose(0, 2, 1, 3)
        scores = jnp.einsum('bghtd,bgsd->bghts', Q, K) * scale
        mask = _sliding_mask(T, T)[None, None, None, :, :]
        neg = jnp.finfo(scores.dtype).min
        scores = jnp.where(mask, scores, neg)
        W = jax.nn.softmax(scores, axis=-1)
        out = jnp.einsum('bghts,bgsd->bghtd', W, V)
        out = out.reshape(B, N_HEAD, T, D_HEAD).transpose(0, 2, 1, 3).reshape(B, T, C)
        return out @ Wo + bo

    def _L0_xattn_ref(query, key, value):
        import jax, jax.numpy as jnp
        import numpy as np
        HIDDEN = 256
        NUM_HEADS = 16
        HEAD_DIM = HIDDEN // NUM_HEADS
        CHUNK = 128
        SCALE = HEAD_DIM ** (-0.5)

        def _chunked_causal_attention(q, k, v):
            B, H, S, D = q.shape
            n_chunks = S // CHUNK
            kc = k.reshape(B, H, n_chunks, CHUNK, D).transpose(2, 0, 1, 3, 4)
            vc = v.reshape(B, H, n_chunks, CHUNK, D).transpose(2, 0, 1, 3, 4)
            j0s = jnp.arange(n_chunks) * CHUNK
            q_idx = jnp.arange(S)[:, None]
            k_off = jnp.arange(CHUNK)[None, :]
            out0 = jnp.zeros_like(q)
            m0 = jnp.full((B, H, S, 1), -jnp.inf, dtype=q.dtype)
            s0 = jnp.zeros((B, H, S, 1), dtype=q.dtype)

            def step(carry, inputs):
                out, m, s = carry
                kj, vj, j0 = inputs
                scores = jnp.einsum('bhqd,bhkd->bhqk', q, kj) * SCALE
                causal = j0 + k_off > q_idx
                scores = jnp.where(causal[None, None], -jnp.inf, scores)
                chunk_max = scores.max(axis=-1, keepdims=True)
                new_m = jnp.maximum(m, chunk_max)
                exp_old = jnp.exp(m - new_m)
                exp_c = jnp.exp(scores - new_m)
                new_s = s * exp_old + exp_c.sum(axis=-1, keepdims=True)
                out = out * (s / new_s) * exp_old + jnp.einsum('bhqk,bhkd->bhqd', exp_c / new_s, vj)
                return ((out, new_m, new_s), None)
            (out, _, _), _ = jax.lax.scan(step, (out0, m0, s0), (kc, vc, j0s))
            return out
        B, S, _ = query.shape
        q = query.reshape(B, S, NUM_HEADS, HEAD_DIM).transpose(0, 2, 1, 3)
        k = key.reshape(B, S, NUM_HEADS, HEAD_DIM).transpose(0, 2, 1, 3)
        v = value.reshape(B, S, NUM_HEADS, HEAD_DIM).transpose(0, 2, 1, 3)
        out = _chunked_causal_attention(q, k, v)
        return out.transpose(0, 2, 1, 3).reshape(B, S, HIDDEN)

    def _L0_ffn_ref(hidden_states, gate_w, sgate_w, w13, w2, shared_gate_up_w, shared_down_w):
        import jax, jax.numpy as jnp
        import numpy as np
        TOP_K = 4

        def _silu_and_mul(gu):
            g, u = jnp.split(gu, 2, axis=-1)
            return jax.nn.silu(g) * u
        B, S, H = hidden_states.shape
        x = hidden_states.reshape(-1, H)
        E = gate_w.shape[0]
        shared = _silu_and_mul(x @ shared_gate_up_w.T) @ shared_down_w.T
        shared = shared * jax.nn.sigmoid(x @ sgate_w.T)
        router_logits = x @ gate_w.T
        routing_weights = jax.nn.softmax(router_logits.astype(jnp.float32), axis=-1)
        topk_w, topk_ids = jax.lax.top_k(routing_weights, TOP_K)

        def body(acc, ew):
            w13_e, w2_e, e = ew
            coef = jnp.sum(jnp.where(topk_ids == e, topk_w, 0.0), axis=-1)
            h = _silu_and_mul(x @ w13_e.T)
            acc = acc + (h @ w2_e.T).astype(jnp.float32) * coef[:, None]
            return (acc, None)
        init = jnp.zeros((x.shape[0], H), dtype=jnp.float32)
        sparse_out, _ = jax.lax.scan(body, init, (w13, w2, jnp.arange(E)))
        out = shared + sparse_out.astype(x.dtype)
        return out.reshape(B, S, H)
    x = x + _L0_attn_ref(_layernorm(x, axis=-1), L0_attn_Wq, L0_attn_bq, L0_attn_Wk, L0_attn_bk, L0_attn_Wv, L0_attn_bv, L0_attn_Wo, L0_attn_bo)
    x = x + _L0_xattn_ref(_layernorm(x, axis=-1), ctx_2048, ctx_2048)
    x = x + _L0_ffn_ref(_layernorm(x, axis=-1), L0_ffn_gate_w, L0_ffn_sgate_w, L0_ffn_w13, L0_ffn_w2, L0_ffn_shared_gate_up_w, L0_ffn_shared_down_w)
    return x

_drawn_inputs = setup_inputs


def setup_inputs(seed=0):
    import zlib

    import numpy as np

    out = dict(_drawn_inputs(seed))
    spreads = {}
    factors = {'L0_attn_Wq': 3.001,
     'L0_attn_bq': 8.0,
     'L0_attn_Wk': 3.007,
     'L0_attn_bk': 8.0,
     'L0_ffn_gate_w': 8.0,
     'L0_ffn_sgate_w': 8.0,
     'L0_ffn_w13': 8.0,
     'L0_ffn_w2': 8.0,
     'L0_ffn_shared_gate_up_w': 5.324,
     'L0_ffn_shared_down_w': 5.342}
    for name, (base, spread) in spreads.items():
        noise = np.random.default_rng([zlib.crc32(name.encode()), seed]).standard_normal(out[name].shape)
        drawn = base * np.exp(spread * noise) if base else spread * noise
        out[name] = jnp.asarray(drawn.astype(out[name].dtype))
    for name, factor in factors.items():
        out[name] = (out[name] * factor).astype(out[name].dtype)
    return out
```

```python
from contextlib import ExitStack

import numpy as np

import concourse.bass as bass
from concourse import mybir

F32 = mybir.dt.float32
F32R = mybir.dt.float32r
BF16 = mybir.dt.bfloat16
U32 = mybir.dt.uint32
U16 = mybir.dt.uint16
ALU = mybir.AluOpType
ACT = mybir.ActivationFunctionType
AX = mybir.AxisListType

B, T, D = 8, 128, 256
NH, DH, NG = 16, 16, 4
PAD = 32
BLK = 4
ROWT = 4
KC = D // 128
QKV = NH * DH + 2 * NG * DH
ROT = NH * DH + NG * DH
TOPK = 4
NE, HE, HS = 16, 176, 704
HID = NE * HE + HS
NC = -(-HID // 128)
RING = 4
PARTS = 3
NCO = NE + 1
HALF = 512
NHALF = B * T // HALF
WROW = KC * 256 + D
SCALE = DH ** -0.5
EPS = 1e-5
MASKED = -1e30


def decoder_layer(nc, x_in, ctx_in, wqkv_in, bqkv_in, wo_in, bo_in, rope_in, masks_in, gate_in,
                  chunks_in, select_in, ident_in, iota_in, out):
    ctx = ExitStack()
    with ctx:
        def sb(name, shape, dt=F32):
            return ctx.enter_context(nc.sbuf_tensor(name, shape, dt))

        def bank(name, dt=F32):
            return ctx.enter_context(nc.psum_tensor(name, [128, 2048 // mybir.dt.size(dt)], dt))

        def sem(name):
            return ctx.enter_context(nc.semaphore(name))

        ident = sb("ident", [128, 128])
        ident_b = sb("ident_b", [128, 128], BF16)
        masks = sb("masks", [128, 2, BLK * 128], BF16)
        rope = sb("rope", [128, 2, ROT])
        wqkv = sb("wqkv", [128, KC, QKV])
        bqkv = sb("bqkv", [128, QKV])
        wo = sb("wo", [128, KC, D])
        bo = sb("bo", [128, D])
        gate = sb("gate", [128, KC, NCO + 1])
        gate_h = sb("gate_h", [128, KC, NCO + 1], F32R)
        gate_l = sb("gate_l", [128, KC, NCO + 1], F32R)
        iota = sb("iota", [128, NE])
        expo = sb("expo", [128, B])
        zero_b = sb("zero_b", [1, HALF], BF16)

        x = sb("x", [128, B + 1, D])
        ctx_sb = sb("ctx_sb", [128, B, D])
        x2 = sb("x2", [128, B, D])
        x3 = sb("x3", [128, B + 1, D])
        stat1 = sb("stat1", [128, B, 6])
        mv1 = sb("mv1", [128, B + 1, 2])
        ve1 = sb("ve1", [128, B])
        rstd1 = sb("rstd1", [128, B + 1])
        xth = sb("xth", [128, KC, (B + 1) * T], F32R)
        xtl = sb("xtl", [128, KC, (B + 1) * T], F32R)

        xn1 = sb("xn1", [128, D])
        xt1 = sb("xt1", [128, KC, 128])
        qkv = sb("qkv", [128, QKV])
        turned = sb("turned", [128, ROT])
        swapped = sb("swapped", [128, ROT])
        q_pad = sb("q_pad", [128, BLK, ROWT, PAD])
        k_pad = sb("k_pad", [128, NG, PAD])
        v_pad = sb("v_pad", [128, NG, PAD])
        qt = sb("qt", [128, BLK, 128])
        kt = sb("kt", [128, 128])
        qc_pad = sb("qc_pad", [128, BLK, ROWT, PAD])
        c_pad = sb("c_pad", [128, BLK, ROWT, PAD])
        qtc = sb("qtc", [128, BLK, 128])
        ktc = sb("ktc", [128, BLK, 128])
        neg_max = sb("neg_max", [128, ROWT, BLK])
        probs = sb("probs", [128, ROWT, BLK, 128])
        probs_t = sb("probs_t", [128, ROWT, BLK, 128])
        values_t = sb("values_t", [128, BLK, 128])
        inv = sb("inv", [128, NH])
        attn = sb("attn", [128, D])
        attn_t = sb("attn_t", [128, KC, 128])
        values_tc = sb("values_tc", [128, BLK, 128])
        inv_c = sb("inv_c", [128, NH])
        attn_c = sb("attn_c", [128, D])
        stat2 = sb("stat2", [128, 2, 6])
        mv2 = sb("mv2", [128, 2, 2])
        ve2 = sb("ve2", [128, 2])
        rstd2 = sb("rstd2", [128, 2])
        xn3 = sb("xn3", [128, D])
        spare = sb("spare", [128, 3])

        logits_t = sb("logits_t", [NCO + 1, B * T])
        logits = sb("logits", [128, B, NCO])
        top_l = sb("top_l", [128, B])
        ex = sb("ex", [128, B, NE])
        ex_g = sb("ex_g", [128, B])
        ex_g1 = sb("ex_g1", [128, B])
        ex_sum = sb("ex_sum", [128, B])
        ex_inv = sb("ex_inv", [128, B])
        top_v = sb("top_v", [128, B, 8])
        top_i = sb("top_i", [128, B, 8], U32)
        top_f = sb("top_f", [128, B, 8])
        picked = sb("picked", [128, TOPK, B, NE])
        coef = sb("coef", [128, B, NCO])
        coef_r = sb("coef_r", [128, 2, B, NCO])
        coef_b = sb("coef_b", [128, B, PARTS, NCO], BF16)
        coef_t = sb("coef_t", [PARTS * NCO, B * T], BF16)

        w_raw = sb("w_raw", [128, RING, WROW])
        w_h = sb("w_h", [128, RING, WROW], F32R)
        w_l = sb("w_l", [128, RING, WROW], F32R)
        sel = sb("sel", [PARTS * NCO, RING, 128], BF16)
        silu = sb("silu", [128, 2, HALF])
        gu = sb("gu", [128, 2, HALF])
        hid = sb("hid", [128, 2, HALF])
        hid_h = sb("hid_h", [128, 2, HALF], F32R)
        hid_l = sb("hid_l", [128, 2, HALF], F32R)
        y_t = sb("y_t", [128, KC, HALF])
        y = sb("y", [128, NHALF * 2, 2, D])

        pb = [bank(f"bank{i}") for i in range(8)]
        ps_s = [pb[g][:, :] for g in range(ROWT)]
        ps_x, ps_q, ps_o, ps_w = pb[4], pb[5], pb[6], pb[7]
        ps_g, ps_u, ps_c, ps_y, ps_t = [pb[0], pb[1]], [pb[2], pb[3]], pb[4], [pb[5], pb[6]], pb[7]

        x_first = sem("x_first")
        x_rest = sem("x_rest")
        ctx_loaded = sem("ctx_loaded")
        ident_loaded = sem("ident_loaded")
        wqkv_loaded = sem("wqkv_loaded")
        rope_loaded = sem("rope_loaded")
        masks_loaded = sem("masks_loaded")
        wo_loaded = sem("wo_loaded")
        gate_loaded = sem("gate_loaded")
        pads_ready = sem("pads_ready")
        ident_b_ready = sem("ident_b_ready")
        gate_h_ready = sem("gate_h_ready")
        gate_l_ready = sem("gate_l_ready")
        stats1_ready = sem("stats1_ready")
        var1_ready = sem("var1_ready")
        rstd1_ready = sem("rstd1_ready")
        xb_ready = sem("xb_ready")
        chain1 = sem("chain1")
        xn1_ready = sem("xn1_ready")
        xt1_psum = sem("xt1_psum")
        xt1_ready = sem("xt1_ready")
        qkv_psum = sem("qkv_psum")
        qkv_ready = sem("qkv_ready")
        rope_step = sem("rope_step")
        v_ready = sem("v_ready")
        qk_ready = sem("qk_ready")
        qkt_psum = sem("qkt_psum")
        qt_ready = sem("qt_ready")
        kt_ready = sem("kt_ready")
        scores_psum = [sem("scores_psum_s"), sem("scores_psum_c")]
        max_step = [sem("max_step_s"), sem("max_step_c")]
        probs_ready = [sem("probs_ready_s"), sem("probs_ready_c")]
        probs_t_psum = [sem("probs_t_psum_s"), sem("probs_t_psum_c")]
        probs_t_act = [sem("probs_t_act_s"), sem("probs_t_act_c")]
        probs_t_dve = [sem("probs_t_dve_s"), sem("probs_t_dve_c")]
        values_psum = [sem("values_psum_s"), sem("values_psum_c")]
        values_taken = [sem("values_taken_s"), sem("values_taken_c")]
        rows_psum = [sem("rows_psum_s"), sem("rows_psum_c")]
        inv_ready = [sem("inv_ready_s"), sem("inv_ready_c")]
        attn_ready = [sem("attn_ready_s"), sem("attn_ready_c")]
        attn_t_psum = sem("attn_t_psum")
        attn_t_ready = sem("attn_t_ready")
        wo_psum = sem("wo_psum")
        x2_ready = sem("x2_ready")
        stat_step = sem("stat_step")
        mv2_ready = sem("mv2_ready")
        ve2_ready = sem("ve2_ready")
        rstd2_ready = sem("rstd2_ready")
        xn2_ready = sem("xn2_ready")
        c_pad_ready = sem("c_pad_ready")
        ct_psum = sem("ct_psum")
        ktc_ready = sem("ktc_ready")
        qc_psum = sem("qc_psum")
        qtc_ready = sem("qtc_ready")
        x3_ready = sem("x3_ready")
        xn3_ready = sem("xn3_ready")
        xt3_psum = sem("xt3_psum")
        xth_ready = sem("xth_ready")
        xtl_ready = sem("xtl_ready")
        lt_psum = sem("lt_psum")
        lt_ready = sem("lt_ready")
        logits_psum = sem("logits_psum")
        route = sem("route")
        shifted_ready = sem("shifted_ready")
        exps_ready = sem("exps_ready")
        coef_ready = sem("coef_ready")
        coef_psum = sem("coef_psum")
        coef_t_ready = sem("coef_t_ready")
        w_loaded = [sem(f"w_loaded{r}") for r in range(RING)]
        wh_ready = sem("wh_ready")
        wl_ready = sem("wl_ready")
        up_psum = sem("up_psum")
        co_psum = sem("co_psum")
        silu_ready = sem("silu_ready")
        gu_ready = sem("gu_ready")
        hid_ready = sem("hid_ready")
        hidh_ready = sem("hidh_ready")
        hidl_ready = sem("hidl_ready")
        down_done = sem("down_done")
        yt_ready = sem("yt_ready")
        y_psum = sem("y_psum")
        y_ready = sem("y_ready")
        y_stored = sem("y_stored")

        block = ctx.enter_context(nc.Block())
        SELF, CROSS = 0, 1

        def store(sp, half, pair):
            m = 2 * half + pair
            sp.wait_ge(y_ready, m + 1)
            b = m * 2
            sp.dma_start(out[b:b + 2].rearrange("b p d -> p b d"), y[:, m, :, :]).then_inc(y_stored, 16)

        @block.sync
        def _(sp):
            sp.dma_start(x[:, 0, :], x_in[0]).then_inc(x_first, 16)
            sp.dma_start(ident[:, :], ident_in).then_inc(ident_loaded, 16)
            sp.dma_start(wqkv[:, :, :], wqkv_in.rearrange("(k p) n -> p k n", p=128)).then_inc(wqkv_loaded, 16)
            sp.dma_start(bqkv[:, :], bqkv_in.partition_broadcast(128)).then_inc(rope_loaded, 16)
            sp.dma_start(rope[:, :, :], rope_in).then_inc(rope_loaded, 16)
            sp.dma_start(masks[:, :, :].bitcast(U16), masks_in).then_inc(masks_loaded, 16)
            sp.dma_start(x[:, 1:B, :], x_in[1:B].rearrange("b p d -> p b d")).then_inc(x_rest, 16)
            sp.dma_start(bo[:, :], bo_in.partition_broadcast(128)).then_inc(wo_loaded, 16)
            sp.dma_start(wo[:, :, :], wo_in.rearrange("(k p) n -> p k n", p=128)).then_inc(wo_loaded, 16)
            sp.dma_start(ctx_sb[:, :, :], ctx_in.rearrange("b p d -> p b d")).then_inc(ctx_loaded, 16)
            sp.dma_start(gate[:, :, :], gate_in.rearrange("(k p) n -> p k n", p=128)).then_inc(gate_loaded, 16)
            sp.dma_start(iota[:, :], iota_in.partition_broadcast(128)).then_inc(gate_loaded, 16)

            def load_chunk(n, c, r):
                if not isinstance(n, int) or n >= RING:
                    sp.wait_ge(wl_ready, n - RING + 1)
                    sp.wait_ge(co_psum, n - RING + 1)
                sp.dma_start(w_raw[:, r, :], chunks_in[bass.ds(c, 1)].rearrange("c p n -> p (c n)")).then_inc(w_loaded[r], 16)
                sp.dma_start(sel[:, r, :].bitcast(U16), select_in[bass.ds(c, 1)].rearrange("c p n -> p (c n)")).then_inc(w_loaded[r], 16)

            for half in range(NHALF):
                for r in range(RING):
                    load_chunk(half * NC + r, r, r)
                if half:
                    for pair in range(2):
                        store(sp, half - 1, pair)
                with sp.Fori(1, NC // RING) as turn:
                    for r in range(RING):
                        load_chunk(turn * RING + (half * NC + r), turn * RING + r, r)
            for pair in range(2):
                store(sp, 1, pair)
            sp.wait_ge(y_stored, 16 * NHALF * 2)

        @block.gpsimd
        def _(pool):
            pool.memset(q_pad[:, :, :, :], 0.0).then_inc(pads_ready, 1)
            pool.memset(k_pad[:, :, :], 0.0).then_inc(pads_ready, 1)
            pool.memset(v_pad[:, :, :], 1.0).then_inc(pads_ready, 1)
            pool.memset(expo[:, :], -0.5).then_inc(pads_ready, 1)
            pool.memset(rstd1[:, B:B + 1], 0.0).then_inc(pads_ready, 1)
            pool.memset(mv1[:, B:B + 1, :], 0.0).then_inc(pads_ready, 1)
            pool.memset(qc_pad[:, :, :, :], 0.0).then_inc(pads_ready, 1)
            pool.memset(c_pad[:, :, :, :], 1.0).then_inc(pads_ready, 1)
            pool.memset(zero_b[:, :], 0.0).then_inc(pads_ready, 1)
            pool.memset(xn3[:, :], 0.0).then_inc(pads_ready, 1)
            pool.memset(x[:, B, :], 0.0).then_inc(pads_ready, 1)
            pool.wait_ge(ident_loaded, 16)
            pool.tensor_copy(ident_b[:, :], ident[:, :]).then_inc(ident_b_ready, 1)
            pool.wait_ge(pads_ready, 11)
            pool.wait_ge(var1_ready, 1)
            pool.tensor_tensor(rstd1[:, 0:1], ve1[:, 0:1], expo[:, 0:1], ALU.pow).then_inc(rstd1_ready, 1)
            pool.wait_ge(var1_ready, 2)
            pool.tensor_tensor(rstd1[:, 1:B], ve1[:, 1:B], expo[:, 1:B], ALU.pow).then_inc(rstd1_ready, 1)
            pool.wait_ge(x_first, 16)
            pool.wait_ge(x_rest, 16)
            pool.wait_ge(wo_loaded, 32)
            for b in range(B):
                ins = pool.tensor_tensor(x2[:, b, :], x[:, b, :], bo[:, :], ALU.add)
            ins.then_inc(xb_ready, 1)
            pool.wait_ge(ctx_loaded, 16)

            def iteration(t, self_on, cross_on):
                if cross_on:
                    pool.wait_ge(wo_psum, t)
                    pool.tensor_copy(c_pad[:, :, :, 0:DH],
                                     ctx_sb[:, bass.ds(t - 1, 1), :].rearrange("p b (j g d) -> p (b j) g d", j=BLK, g=ROWT)
                                     ).then_inc(c_pad_ready, 1)
                pool.wait_ge(ve2_ready, t + 1)
                rows = slice(0 if cross_on else 1, 2 if self_on else 1)
                pool.tensor_tensor(rstd2[:, rows], ve2[:, rows], expo[:, rows], ALU.pow).then_inc(rstd2_ready, 1)

            iteration(0, True, False)
            with pool.Fori(1, B) as t:
                iteration(t, True, True)
            iteration(B, False, True)

            def low_part(n, r):
                pool.wait_ge(wh_ready, n + 1)
                pool.tensor_tensor(w_l[:, r, :], w_raw[:, r, :], w_h[:, r, :].bitcast(F32), ALU.subtract
                                   ).then_inc(wl_ready, 1)

            with pool.Fori(0, NHALF * NC, RING) as n:
                for r in range(RING):
                    low_part(n + r, r)

        @block.scalar
        def _(act):
            def front_a(f):
                act.wait_ge(xt1_psum, f + 1)
                act.activation(xt1[:, :, :], ps_x[:, 0:KC * 128].rearrange("p (k n) -> p k n", k=KC), ACT.Copy
                               ).then_inc(xt1_ready, 1)

            def front_c(f):
                act.wait_ge(qkt_psum, f + 1)
                act.activation(qt[:, :, :], ps_q[:, :].rearrange("p (j n) -> p j n", j=BLK), ACT.Copy, scale=SCALE
                               ).then_inc(qt_ready, 1)

            def cross_q(c):
                act.wait_ge(qc_psum, c + 1)
                act.activation(qtc[:, :, :], ps_q[:, :].rearrange("p (j n) -> p j n", j=BLK), ACT.Copy, scale=SCALE
                               ).then_inc(qtc_ready, 1)

            def exps(kind, b, u):
                for g in (2 * u, 2 * u + 1):
                    act.wait_ge(max_step[kind], 4 * b + g + 1)
                    for j in range(BLK):
                        ins = act.activation(probs[:, g, j, :], ps_s[g][:, 128 * j:128 * j + 128], ACT.Exp,
                                             bias=neg_max[:, g, j:j + 1])
                ins.then_inc(probs_ready[kind], 1)

            def take_probs_t(kind, b, u):
                act.wait_ge(probs_t_psum[kind], 2 * b + u + 1)
                act.activation(probs_t[:, 2 * u, :, :], ps_s[2 * u].rearrange("p (j n) -> p j n", j=BLK), ACT.Copy
                               ).then_inc(probs_t_act[kind], 1)

            def take_values(kind, b):
                act.wait_ge(values_psum[kind], 2 * b + 2)
                act.activation((values_t if kind == SELF else values_tc)[:, :, :],
                               ps_o[:, :].rearrange("p (j n) -> p j n", j=BLK), ACT.Copy).then_inc(values_taken[kind], 1)

            def take_attn_t(b):
                act.wait_ge(attn_t_psum, b + 1)
                act.activation(attn_t[:, :, :], ps_x[:, 0:KC * 128].rearrange("p (k n) -> p k n", k=KC), ACT.Copy
                               ).then_inc(attn_t_ready, 1)

            def take_xth(slot):
                act.wait_ge(xt3_psum, slot + 1)
                act.activation(xth[:, :, bass.ds(slot * T, T)],
                               ps_x[:, 0:KC * 128].rearrange("p (k n) -> p k n", k=KC), ACT.Copy
                               ).then_inc(xth_ready, 1)

            def iteration(t, self_on, cross_on):
                if self_on:
                    exps(SELF, t, 0)
                if cross_on:
                    take_xth(t - 1)
                    cross_q(t - 1)
                if self_on:
                    exps(SELF, t, 1)
                    take_probs_t(SELF, t, 0)
                if cross_on:
                    exps(CROSS, t - 1, 0)
                if self_on:
                    take_probs_t(SELF, t, 1)
                    front_a(t + 1)
                if cross_on:
                    exps(CROSS, t - 1, 1)
                    take_probs_t(CROSS, t - 1, 0)
                if self_on:
                    take_values(SELF, t)
                if cross_on:
                    take_probs_t(CROSS, t - 1, 1)
                if self_on:
                    take_attn_t(t)
                    front_c(t + 1)
                if cross_on:
                    take_values(CROSS, t - 1)

            front_a(0)
            front_c(0)
            iteration(0, True, False)
            with act.Fori(1, B) as t:
                iteration(t, True, True)
            iteration(B, False, True)
            take_xth(B)

            def high_part(n, r, m):
                act.wait_ge(w_loaded[r], 32 * (m + 1))
                if not isinstance(n, int) or n >= RING:
                    act.wait_ge(down_done, n - RING + 1)
                act.activation(w_h[:, r, :], w_raw[:, r, :], ACT.Copy).then_inc(wh_ready, 1)

            high_part(0, 0, 0)
            high_part(1, 1, 0)

            act.wait_ge(lt_psum, 1)
            act.activation(logits_t[:, 0:HALF], pb[0][0:NCO + 1, :], ACT.Copy).then_inc(lt_ready, 1)
            act.wait_ge(lt_psum, 2)
            act.activation(logits_t[:, HALF:], pb[1][0:NCO + 1, :], ACT.Copy).then_inc(lt_ready, 1)
            act.wait_ge(shifted_ready, 1)
            act.activation(ex[:, :, :], ex[:, :, :], ACT.Exp).then_inc(exps_ready, 1)
            act.activation(ex_g[:, :], logits[:, :, NE], ACT.Exp, scale=-1.0).then_inc(exps_ready, 1)
            act.wait_ge(coef_psum, 1)
            act.activation(coef_t[:, :], pb[3][0:PARTS * NCO, :].bitcast(BF16), ACT.Copy).then_inc(coef_t_ready, 1)

            def chunk(n, k, q, ahead=True):
                if ahead:
                    r = (k + 2) % RING
                    high_part(n + 2, r, q + (k + 2) // RING)
                act.wait_ge(up_psum, 2 * n + 1)
                if not isinstance(n, int) or n >= 2:
                    act.wait_ge(gu_ready, n - 1)
                act.activation(silu[:, k % 2, :], ps_g[k % 2][:, :], ACT.Silu).then_inc(silu_ready, 1)
                act.wait_ge(hid_ready, n + 1)
                if not isinstance(n, int) or n >= 2:
                    act.wait_ge(down_done, n - 1)
                act.activation(hid_h[:, k % 2, :], hid[:, k % 2, :], ACT.Copy).then_inc(hidh_ready, 1)

            turns = NC // RING
            for half in range(NHALF):
                if half == 0:
                    for k in range(RING):
                        chunk(k, k, 0)
                    first = 1
                else:
                    first = 0
                with act.Fori(first, turns - 1) as i:
                    q = half * turns + i
                    for k in range(RING):
                        chunk(q * RING + k, k, q)
                q = half * turns + turns - 1
                for k in range(RING):
                    chunk(q * RING + k, k, q, ahead=half == 0 or k < RING - 2)
                act.wait_ge(down_done, (half + 1) * NC)
                act.activation(y_t[:, 0, :], ps_y[0][:, :], ACT.Copy).then_inc(yt_ready, 1)

        @block.vector
        def _(dve):
            def one(ap, i):
                return ap[:, bass.ds(i, 1), :].rearrange("p b d -> p (b d)")

            links = [0]

            def link(ins):
                links[0] += 1
                ins.then_inc(chain1, 1)
                dve.wait_ge(chain1, links[0])

            dve.wait_ge(x_first, 16)
            link(dve.bn_stats(stat1[:, 0, :], x[:, 0, :]))
            dve.wait_ge(pads_ready, 11)
            link(dve.bn_aggr(mv1[:, 0, :], stat1[:, 0, :]))
            dve.tensor_scalar(ve1[:, 0:1], mv1[:, 0, 1:2], EPS, None, ALU.add).then_inc(var1_ready, 1)
            dve.wait_ge(x_rest, 16)
            for b in range(1, B):
                dve.bn_stats(stat1[:, b, :], x[:, b, :]).then_inc(stats1_ready, 1)
            for b in range(1, B):
                dve.wait_ge(stats1_ready, b)
                dve.bn_aggr(mv1[:, b, :], stat1[:, b, :]).then_inc(stats1_ready, 1)
            dve.wait_ge(stats1_ready, 2 * (B - 1))
            dve.tensor_scalar(ve1[:, 1:B], mv1[:, 1:B, 1], EPS, None, ALU.add).then_inc(var1_ready, 1)

            def front_n(f):
                dve.wait_ge(xt1_psum, f)
                dve.tensor_scalar(xn1[:, :], one(x, f), mv1[:, bass.ds(f, 1), 0], rstd1[:, bass.ds(f, 1)], ALU.subtract, ALU.mult).then_inc(xn1_ready, 1)

            def front_r(f):
                dve.wait_ge(qkv_psum, f + 1)
                dve.tensor_tensor(qkv[:, :], ps_w[:, 0:QKV], bqkv[:, :], ALU.add).then_inc(qkv_ready, 1)
                dve.wait_ge(qkv_ready, f + 1)
                halves = qkv[:, 0:ROT].rearrange("p (h s i) -> p h s i", s=2, i=DH // 2)
                sines = rope[:, 1, :].rearrange("p (h s i) -> p h s i", s=2, i=DH // 2)
                turn = swapped[:, :].rearrange("p (h s i) -> p h s i", s=2, i=DH // 2)
                dve.tensor_tensor(turned[:, :], qkv[:, 0:ROT], rope[:, 0, :], ALU.mult).then_inc(rope_step, 1)
                dve.tensor_tensor(turn[:, :, 0, :], halves[:, :, 1, :], sines[:, :, 0, :], ALU.mult).then_inc(rope_step, 1)
                dve.tensor_tensor(turn[:, :, 1, :], halves[:, :, 0, :], sines[:, :, 1, :], ALU.mult).then_inc(rope_step, 1)
                dve.tensor_copy(v_pad[:, :, 0:DH], qkv[:, ROT:QKV].rearrange("p (g d) -> p g d", g=NG)
                                ).then_inc(v_ready, 1)
                dve.wait_ge(rope_step, 3 * (f + 1))
                nq = NH * DH
                dve.tensor_tensor(q_pad[:, :, :, 0:DH].rearrange("p j g d -> p g j d"),
                                  turned[:, 0:nq].rearrange("p (g j d) -> p g j d", g=NG, j=BLK),
                                  swapped[:, 0:nq].rearrange("p (g j d) -> p g j d", g=NG, j=BLK), ALU.add
                                  ).then_inc(qk_ready, 1)
                dve.tensor_tensor(k_pad[:, :, 0:DH],
                                  turned[:, nq:ROT].rearrange("p (g d) -> p g d", g=NG),
                                  swapped[:, nq:ROT].rearrange("p (g d) -> p g d", g=NG), ALU.add).then_inc(qk_ready, 1)

            def front_k(f):
                dve.wait_ge(qkt_psum, f + 1)
                dve.tensor_copy(kt[:, :], ps_w[:, 0:128]).then_inc(kt_ready, 1)

            def row_max(kind, b, u):
                dve.wait_ge(scores_psum[kind], 2 * b + u + 1)
                for g in (2 * u, 2 * u + 1):
                    dve.tensor_reduce(neg_max[:, g, :], ps_s[g].rearrange("p (j n) -> p j n", j=BLK), AX.X, ALU.max,
                                      negate=True).then_inc(max_step[kind], 1)

            def take_probs_t(kind, b, u):
                dve.wait_ge(probs_t_psum[kind], 2 * b + u + 1)
                dve.tensor_copy(probs_t[:, 2 * u + 1, :, :], ps_s[2 * u + 1].rearrange("p (j n) -> p j n", j=BLK)
                                ).then_inc(probs_t_dve[kind], 1)

            def normalise(kind, b, inverse, result):
                dve.wait_ge(rows_psum[kind], b + 1)
                heads = ps_o[:, :].rearrange("p (h c) -> p h c", h=NH)
                dve.reciprocal(inverse[:, :], heads[:, :, DH]).then_inc(inv_ready[kind], 1)
                dve.wait_ge(inv_ready[kind], b + 1)
                if kind == SELF:
                    heads = heads.rearrange("p (j g) c -> p j g c", j=BLK)
                    dve.tensor_tensor(result[:, :].rearrange("p (g j d) -> p j g d", g=NG, j=BLK), heads[:, :, :, 0:DH],
                                      inverse[:, :].rearrange("p (j g) -> p j g", j=BLK).unsqueeze(3).broadcast_to([128, BLK, NG, DH]),
                                      ALU.mult).then_inc(attn_ready[kind], 1)
                else:
                    dve.tensor_tensor(result[:, :].rearrange("p (h d) -> p h d", h=NH), heads[:, :, 0:DH],
                                      inverse[:, :].unsqueeze(2).broadcast_to([128, NH, DH]), ALU.mult
                                      ).then_inc(attn_ready[kind], 1)

            def carry_wait(i):
                dve.memset(spare[:, i:i + 1], 0.0)

            def iteration(t, self_on, cross_on):
                if self_on:
                    row_max(SELF, t, 0)
                    row_max(SELF, t, 1)
                if cross_on:
                    take_xtl(t - 1)
                    dve.wait_ge(ct_psum, t)
                    dve.tensor_copy(ktc[:, :, :], ps_x[:, :].rearrange("p (j n) -> p j n", j=BLK)).then_inc(ktc_ready, 1)
                if self_on:
                    front_n(t + 1)
                    take_probs_t(SELF, t, 0)
                if cross_on:
                    row_max(CROSS, t - 1, 0)
                if self_on:
                    take_probs_t(SELF, t, 1)
                if cross_on:
                    row_max(CROSS, t - 1, 1)
                    take_probs_t(CROSS, t - 1, 0)
                if self_on:
                    normalise(SELF, t, inv, attn)
                if cross_on:
                    take_probs_t(CROSS, t - 1, 1)
                if self_on:
                    front_r(t + 1)
                    front_k(t + 1)
                if cross_on:
                    normalise(CROSS, t - 1, inv_c, attn_c)
                    dve.wait_ge(attn_ready[CROSS], t)
                    dve.tensor_tensor(one(x3, t), attn_c[:, :], one(x2, t - 1), ALU.add).then_inc(x3_ready, 1)
                if self_on:
                    dve.wait_ge(wo_psum, t + 1)
                    if isinstance(t, int):
                        dve.wait_ge(xb_ready, 1)
                    dve.tensor_tensor(one(x2, t), ps_w[:, 0:D], one(x2, t), ALU.add).then_inc(x2_ready, 1)
                if cross_on:
                    dve.wait_ge(x3_ready, t)
                    carry_wait(0)
                    dve.bn_stats(stat2[:, 0, :], one(x3, t)).then_inc(stat_step, 1)
                if self_on:
                    dve.wait_ge(x2_ready, t + 1)
                    carry_wait(1)
                    dve.bn_stats(stat2[:, 1, :], one(x2, t)).then_inc(stat_step, 1)
                dve.wait_ge(stat_step, 2 * t + 1 if self_on else 2 * t)
                carry_wait(2)
                if cross_on:
                    dve.bn_aggr(mv2[:, 0, :], stat2[:, 0, :]).then_inc(mv2_ready, 1)
                if self_on:
                    dve.bn_aggr(mv2[:, 1, :], stat2[:, 1, :]).then_inc(mv2_ready, 1)
                rows = slice(0 if cross_on else 1, 2 if self_on else 1)
                dve.wait_ge(mv2_ready, 2 * t + 1 if self_on else 2 * t)
                dve.tensor_scalar(ve2[:, rows], mv2[:, rows, 1], EPS, None, ALU.add).then_inc(ve2_ready, 1)
                dve.wait_ge(rstd2_ready, t + 1)
                if cross_on:
                    dve.tensor_scalar(xn3[:, :], one(x3, t), mv2[:, 0, 0:1], rstd2[:, 0:1], ALU.subtract, ALU.mult
                                      ).then_inc(xn3_ready, 1)
                if self_on:
                    dve.tensor_scalar(qc_pad[:, :, :, 0:DH],
                                      one(x2, t).rearrange("p (j g d) -> p j g d", j=BLK, g=ROWT),
                                      mv2[:, 1, 0:1], rstd2[:, 1:2], ALU.subtract, ALU.mult).then_inc(xn2_ready, 1)

            def take_xtl(slot):
                dve.wait_ge(xth_ready, slot + 1)
                cols = bass.ds(slot * T, T)
                dve.tensor_tensor(xtl[:, :, cols], ps_x[:, 0:KC * 128].rearrange("p (k n) -> p k n", k=KC),
                                  xth[:, :, cols].bitcast(F32), ALU.subtract).then_inc(xtl_ready, 1)

            dve.wait_ge(rstd1_ready, 1)
            front_n(0)
            dve.wait_ge(rope_loaded, 32)
            front_r(0)
            front_k(0)
            dve.wait_ge(rstd1_ready, 2)
            iteration(0, True, False)
            with dve.Fori(1, B) as t:
                iteration(t, True, True)
            iteration(B, False, True)
            dve.wait_ge(gate_loaded, 32)
            dve.tensor_copy(gate_h[:, :, :], gate[:, :, :]).then_inc(gate_h_ready, 1)
            dve.wait_ge(gate_h_ready, 1)
            dve.tensor_tensor(gate_l[:, :, :], gate[:, :, :], gate_h[:, :, :].bitcast(F32), ALU.subtract
                              ).then_inc(gate_l_ready, 1)
            take_xtl(B)

            def over(ap, n):
                return ap.unsqueeze(2).broadcast_to([128, B, n])

            dve.wait_ge(logits_psum, 1)
            link(dve.tensor_copy(logits[:, :, :],
                                 pb[2][:, 0:B * (NCO + 1)].rearrange("p (b e) -> p b e", b=B)[:, :, 0:NCO]))
            link(dve.tensor_reduce(top_l[:, :], logits[:, :, 0:NE], AX.X, ALU.max))
            dve.tensor_tensor(ex[:, :, :], logits[:, :, 0:NE], over(top_l[:, :], NE), ALU.subtract
                              ).then_inc(shifted_ready, 1)
            dve.wait_ge(exps_ready, 2)
            dve.tensor_scalar(ex_g1[:, :], ex_g[:, :], 1.0, None, ALU.add).then_inc(chain1, 1)
            dve.tensor_reduce(ex_sum[:, :], ex[:, :, :], AX.X, ALU.add).then_inc(chain1, 1)
            links[0] += 2
            for b in range(B):
                dve.max(top_v[:, b, :], ex[:, b, :]).then_inc(route, 1)
            for b in range(B):
                dve.wait_ge(route, b + 1)
                dve.max_index(top_i[:, b, :], top_v[:, b, :], ex[:, b, :]).then_inc(route, 1)
            dve.wait_ge(chain1, links[0])
            dve.reciprocal(ex_inv[:, :], ex_sum[:, :]).then_inc(chain1, 1)
            dve.reciprocal(coef[:, :, NE], ex_g1[:, :]).then_inc(chain1, 1)
            links[0] += 2
            dve.wait_ge(route, 2 * B)
            link(dve.tensor_copy(top_f[:, :, :], top_i[:, :, :]))
            for k in range(TOPK):
                dve.tensor_tensor(picked[:, k, :, :], iota[:, :].unsqueeze(1).broadcast_to([128, B, NE]), over(top_f[:, :, k], NE),
                                  ALU.is_equal).then_inc(chain1, 1)
                links[0] += 1
            dve.wait_ge(chain1, links[0])
            for k in range(TOPK):
                dve.tensor_tensor(picked[:, k, :, :], picked[:, k, :, :], over(top_v[:, :, k], NE), ALU.mult
                                  ).then_inc(chain1, 1)
                links[0] += 1
            dve.wait_ge(chain1, links[0])
            link(dve.tensor_tensor(picked[:, 0:2, :, :], picked[:, 0:2, :, :], picked[:, 2:4, :, :], ALU.add))
            link(dve.tensor_tensor(picked[:, 0, :, :], picked[:, 0, :, :], picked[:, 1, :, :], ALU.add))
            link(dve.tensor_tensor(coef[:, :, 0:NE], picked[:, 0, :, :], over(ex_inv[:, :], NE), ALU.mult))
            link(dve.tensor_copy(coef_b[:, :, 0, :], coef[:, :, :]))
            link(dve.tensor_tensor(coef_r[:, 0, :, :], coef[:, :, :], coef_b[:, :, 0, :], ALU.subtract))
            link(dve.tensor_copy(coef_b[:, :, 1, :], coef_r[:, 0, :, :]))
            link(dve.tensor_tensor(coef_r[:, 1, :, :], coef_r[:, 0, :, :], coef_b[:, :, 1, :], ALU.subtract))
            dve.tensor_copy(coef_b[:, :, 2, :], coef_r[:, 1, :, :]).then_inc(coef_ready, 1)

            def chunk(n, k):
                dve.wait_ge(silu_ready, n + 1)
                dve.wait_ge(up_psum, 2 * n + 2)
                dve.tensor_tensor(gu[:, k % 2, :], silu[:, k % 2, :], ps_u[k % 2][:, :], ALU.mult).then_inc(gu_ready, 1)
                dve.wait_ge(gu_ready, n + 1)
                dve.wait_ge(co_psum, n + 1)
                if not isinstance(n, int) or n >= 2:
                    dve.wait_ge(hidl_ready, n - 1)
                dve.tensor_tensor(hid[:, k % 2, :], gu[:, k % 2, :], ps_c[:, :], ALU.mult).then_inc(hid_ready, 1)
                dve.wait_ge(hidh_ready, n + 1)
                dve.tensor_tensor(hid_l[:, k % 2, :], hid[:, k % 2, :], hid_h[:, k % 2, :].bitcast(F32), ALU.subtract
                                  ).then_inc(hidl_ready, 1)

            def finish(half):
                dve.wait_ge(down_done, (half + 1) * NC)
                dve.tensor_copy(y_t[:, 1, :], ps_y[1][:, :]).then_inc(yt_ready, 1)

            def sum_rows(half, pair):
                m = 2 * half + pair
                dve.wait_ge(y_psum, m + 1)
                dve.tensor_tensor(y[:, m, :, :], ps_t[:, :].rearrange("p (b d) -> p b d", b=2),
                                  x3[:, 2 * m + 1:2 * m + 3, :], ALU.add).then_inc(y_ready, 1)

            for k in range(RING):
                chunk(k, k)
            with dve.Fori(RING, NC, RING) as n:
                for k in range(RING):
                    chunk(n + k, k)
            finish(0)
            for k in range(RING):
                chunk(NC + k, k)
                if k < 2:
                    sum_rows(0, k)
            with dve.Fori(NC + RING, 2 * NC, RING) as n:
                for k in range(RING):
                    chunk(n + k, k)
            finish(1)
            for pair in range(2):
                sum_rows(1, pair)

        @block.tensor
        def _(pe):
            def front_a(f):
                pe.wait_ge(xn1_ready, f + 1)
                if not isinstance(f, int) or f >= 1:
                    pe.wait_ge(attn_t_ready, f - 1)
                for k in range(KC):
                    ins = pe.transpose(ps_x[:, 128 * k:128 * k + 128], xn1[:, 128 * k:128 * k + 128], ident[:, :])
                ins.then_inc(xt1_psum, 1)

            def front_b(f):
                pe.wait_ge(xt1_ready, f + 1)
                if not isinstance(f, int) or f >= 2:
                    pe.wait_ge(x2_ready, f - 1)
                for k in range(KC):
                    ins = pe.matmul(ps_w[:, 0:QKV], xt1[:, k, :], wqkv[:, k, :], start=k == 0, stop=k == KC - 1)
                ins.then_inc(qkv_psum, 1)

            def front_c(f):
                pe.wait_ge(qk_ready, 2 * f + 2)
                if not isinstance(f, int) or f >= 2:
                    pe.wait_ge(qtc_ready, f - 1)
                for j in range(BLK):
                    pe.transpose(ps_q[:, 128 * j:128 * j + 128], q_pad[:, j, :, :].rearrange("p g d -> p (g d)"),
                                 ident[:, :])
                pe.transpose(ps_w[:, 0:128], k_pad[:, :, :].rearrange("p g d -> p (g d)"), ident[:, :]
                             ).then_inc(qkt_psum, 1)

            def scores(kind, b, u):
                queries = qt if kind == SELF else qtc
                for g in (2 * u, 2 * u + 1):
                    pe.matmul(ps_s[g], ident_b[:, :], masks[:, kind, :], start=True, stop=False)
                for j in range(BLK):
                    for g in (2 * u, 2 * u + 1):
                        rows = slice(PAD * g, PAD * g + DH)
                        keys = kt[rows, :] if kind == SELF else ktc[rows, j, :]
                        ins = pe.matmul(ps_s[g][:, 128 * j:128 * j + 128], queries[rows, j, :], keys,
                                        start=False, stop=j == BLK - 1)
                ins.then_inc(scores_psum[kind], 1)

            def transpose_probs(kind, b, u):
                pe.wait_ge(probs_ready[kind], 2 * b + u + 1)
                for g in (2 * u, 2 * u + 1):
                    for j in range(BLK):
                        ins = pe.transpose(ps_s[g][:, 128 * j:128 * j + 128], probs[:, g, j, :], ident[:, :])
                ins.then_inc(probs_t_psum[kind], 1)

            def values(kind, b, u):
                pe.wait_ge(probs_t_act[kind], 2 * b + u + 1)
                pe.wait_ge(probs_t_dve[kind], 2 * b + u + 1)
                for g in (2 * u, 2 * u + 1):
                    out_rows = slice(PAD * g, PAD * g + PAD)
                    if kind == SELF:
                        ins = pe.matmul(ps_o[out_rows, :], v_pad[:, g, :],
                                        probs_t[:, g, :, :].rearrange("p j n -> p (j n)"), start=True, stop=True)
                        continue
                    for j in range(BLK):
                        ins = pe.matmul(ps_o[out_rows, 128 * j:128 * j + 128], c_pad[:, j, g, :], probs_t[:, g, j, :],
                                        start=True, stop=True)
                ins.then_inc(values_psum[kind], 1)

            def turn_values(kind, b):
                pe.wait_ge(values_taken[kind], b + 1)
                for j in range(BLK):
                    ins = pe.transpose(ps_o[:, 128 * j:128 * j + 128], (values_t if kind == SELF else values_tc)[:, j, :],
                                       ident[:, :])
                ins.then_inc(rows_psum[kind], 1)

            def project(b):
                pe.wait_ge(attn_t_ready, b + 1)
                pe.wait_ge(kt_ready, b + 2)
                for k in range(KC):
                    ins = pe.matmul(ps_w[:, 0:D], attn_t[:, k, :], wo[:, k, :], start=k == 0, stop=k == KC - 1)
                ins.then_inc(wo_psum, 1)

            def third_norm(slot):
                if isinstance(slot, int) and slot > 0:
                    pe.wait_ge(xn3_ready, slot)
                for k in range(KC):
                    ins = pe.transpose(ps_x[:, 128 * k:128 * k + 128], xn3[:, 128 * k:128 * k + 128], ident[:, :])
                ins.then_inc(xt3_psum, 1)

            def iteration(t, self_on, cross_on):
                c = t - 1
                if self_on:
                    pe.wait_ge(qt_ready, t + 1)
                    pe.wait_ge(kt_ready, t + 1)
                    scores(SELF, t, 0)
                    scores(SELF, t, 1)
                if cross_on:
                    pe.wait_ge(attn_t_ready, t)
                    pe.wait_ge(xn2_ready, t)
                    third_norm(t - 1)
                    pe.wait_ge(qt_ready, t + 1)
                    for j in range(BLK):
                        ins = pe.transpose(ps_q[:, 128 * j:128 * j + 128],
                                           qc_pad[:, j, :, :].rearrange("p g d -> p (g d)"), ident[:, :])
                    ins.then_inc(qc_psum, 1)
                if self_on:
                    transpose_probs(SELF, t, 0)
                if cross_on:
                    pe.wait_ge(c_pad_ready, t)
                    pe.wait_ge(xtl_ready, t)
                    for j in range(BLK):
                        ins = pe.transpose(ps_x[:, 128 * j:128 * j + 128],
                                           c_pad[:, j, :, :].rearrange("p g d -> p (g d)"), ident[:, :])
                    ins.then_inc(ct_psum, 1)
                    pe.wait_ge(qtc_ready, t)
                    pe.wait_ge(ktc_ready, t)
                    if self_on:
                        pe.wait_ge(probs_t_act[SELF], 2 * t + 1)
                        pe.wait_ge(probs_t_dve[SELF], 2 * t + 1)
                    scores(CROSS, c, 0)
                if self_on:
                    transpose_probs(SELF, t, 1)
                    if cross_on:
                        pe.wait_ge(x2_ready, t)
                    values(SELF, t, 0)
                if cross_on:
                    if self_on:
                        pe.wait_ge(probs_t_act[SELF], 2 * t + 2)
                        pe.wait_ge(probs_t_dve[SELF], 2 * t + 2)
                    scores(CROSS, c, 1)
                if self_on:
                    front_a(t + 1)
                if cross_on:
                    transpose_probs(CROSS, c, 0)
                if self_on:
                    values(SELF, t, 1)
                    front_b(t + 1)
                    turn_values(SELF, t)
                if cross_on:
                    transpose_probs(CROSS, c, 1)
                    pe.wait_ge(attn_ready[SELF], t + 1 if self_on else t)
                    values(CROSS, c, 0)
                if self_on:
                    pe.wait_ge(attn_ready[SELF], t + 1)
                    pe.wait_ge(xt1_ready, t + 2)
                    for k in range(KC):
                        ins = pe.transpose(ps_x[:, 128 * k:128 * k + 128], attn[:, 128 * k:128 * k + 128], ident[:, :])
                    ins.then_inc(attn_t_psum, 1)
                    front_c(t + 1)
                if cross_on:
                    values(CROSS, c, 1)
                if self_on:
                    project(t)
                if cross_on:
                    turn_values(CROSS, c)

            pe.wait_ge(ident_loaded, 16)
            pe.wait_ge(pads_ready, 11)
            front_a(0)
            pe.wait_ge(wqkv_loaded, 16)
            front_b(0)
            front_c(0)
            pe.wait_ge(ident_b_ready, 1)
            pe.wait_ge(masks_loaded, 16)
            pe.wait_ge(wo_loaded, 32)
            iteration(0, True, False)
            with pe.Fori(1, B) as t:
                iteration(t, True, True)
            iteration(B, False, True)
            third_norm(B)

            def three(outs, pairs_h, pairs_l, first, last):
                n = len(pairs_h)
                todo = [(pairs_h[k][0], pairs_h[k][1]) for k in range(n)]
                todo += [(pairs_h[k][0], pairs_l[k][1]) for k in range(n)]
                todo += [(pairs_l[k][0], pairs_h[k][1]) for k in range(n)]
                for i, (w, m) in enumerate(todo):
                    ins = pe.matmul(outs, w, m, start=first and i == 0, stop=last and i == len(todo) - 1,
                                    skip_group_check=not (first and last))
                return ins

            pe.wait_ge(gate_l_ready, 1)
            pe.wait_ge(xtl_ready, B + 1)
            for half in range(NHALF):
                cols = slice(T + half * HALF, T + (half + 1) * HALF)
                three(pb[half][0:NCO + 1, :],
                      [(gate_h[:, k, :], xth[:, k, cols]) for k in range(KC)],
                      [(gate_l[:, k, :], xtl[:, k, cols]) for k in range(KC)], True, True).then_inc(lt_psum, 1)
            pe.wait_ge(lt_ready, 2)
            for b in range(B):
                ins = pe.transpose(pb[2][:, (NCO + 1) * b:(NCO + 1) * (b + 1)], logits_t[:, T * b:T * b + T],
                                   ident[0:NCO + 1, 0:NCO + 1])
            ins.then_inc(logits_psum, 1)
            pe.wait_ge(coef_ready, 1)
            for b in range(B):
                ins = pe.transpose(pb[3][0:PARTS * NCO, :].bitcast(BF16)[:, T * b:T * b + T],
                                   coef_b[:, b, :, :].rearrange("p s e -> p (s e)"), ident_b[:, :])
            ins.then_inc(coef_psum, 1)
            pe.wait_ge(coef_t_ready, 1)

            def up(n, k, cols, tokens, early=False):
                pe.wait_ge(wl_ready, n + 1)
                for part in range(2):
                    if not early:
                        pe.wait_ge([silu_ready, gu_ready][part], n - 1)
                    rows = [slice(256 * c + 128 * part, 256 * c + 128 * part + 128) for c in range(KC)]
                    three([ps_g, ps_u][part][k % 2][:, :],
                          [(w_h[:, k, rows[c]], xth[:, c, cols]) for c in range(KC)],
                          [(w_l[:, k, rows[c]], xtl[:, c, cols]) for c in range(KC)], True, True).then_inc(up_psum, 1)
                if not early:
                    pe.wait_ge(hid_ready, n)
                pe.matmul(ps_c[:, :], sel[:, k, :], coef_t[:, tokens], start=True, stop=True).then_inc(co_psum, 1)

            def down(n, k, last=False):
                pe.wait_ge(hidl_ready, n + 1)
                for m in range(KC):
                    rows = slice(KC * 256 + 128 * m, KC * 256 + 128 * m + 128)
                    ins = three(ps_y[m][:, :], [(w_h[:, k, rows], hid_h[:, k % 2, :])],
                                [(w_l[:, k, rows], hid_l[:, k % 2, :])], False, last)
                ins.then_inc(down_done, 1)

            def open_rows():
                for m in range(KC):
                    pe.matmul(ps_y[m][:, :], zero_b[0:1, 0:128], zero_b[0:1, :], start=True, stop=False,
                              skip_group_check=True)

            def turn_rows(half, pair):
                m = 2 * half + pair
                pe.wait_ge(yt_ready, 2 * half + 2)
                if m:
                    pe.wait_ge(y_ready, m)
                for i in range(2):
                    for k in range(KC):
                        at = T * (2 * pair + i)
                        ins = pe.transpose(ps_t[:, D * i + 128 * k:D * i + 128 * k + 128], y_t[:, k, at:at + T],
                                           ident[:, :])
                ins.then_inc(y_psum, 1)

            def columns(half):
                return slice(T + half * HALF, T + (half + 1) * HALF), slice(half * HALF, (half + 1) * HALF)

            up(0, 0, *columns(0), early=True)
            for half in range(NHALF):
                if half:
                    pe.wait_ge(yt_ready, 2 * half)
                open_rows()
                for k in range(RING):
                    if half == 0 or k:
                        pass
                    up(half * NC + k + 1, (k + 1) % RING, *columns(half), early=False)
                    down(half * NC + k, k)
                    if half and k < 2:
                        turn_rows(half - 1, k)
                with pe.Fori(half * NC + RING, (half + 1) * NC - RING, RING) as n:
                    for k in range(RING):
                        up(n + k + 1, (k + 1) % RING, *columns(half))
                        down(n + k, k)
                for k in range(RING):
                    n = (half + 1) * NC - RING + k
                    if k < RING - 1:
                        up(n + 1, k + 1, *columns(half))
                    elif half + 1 < NHALF:
                        up(n + 1, 0, *columns(half + 1))
                    down(n, k, last=k == RING - 1)
            for pair in range(2):
                turn_rows(NHALF - 1, pair)


def bf16_bits(table):
    return (table.astype(np.float32).view(np.uint32) >> 16).astype(np.uint16)


def lay_out(inputs):
    a = {k: np.asarray(v) for k, v in inputs.items()}
    f = np.float32
    got = {"x_in": a["x"], "ctx_in": a["ctx_2048"]}
    got["wqkv_in"] = np.concatenate([a["L0_attn_Wq"], a["L0_attn_Wk"], a["L0_attn_Wv"]], axis=1)
    got["bqkv_in"] = np.concatenate([a["L0_attn_bq"], a["L0_attn_bk"], a["L0_attn_bv"]])
    got["wo_in"] = a["L0_attn_Wo"]
    got["bo_in"] = a["L0_attn_bo"]
    half = DH // 2
    freq = (1.0 / f(10000.0) ** (np.arange(half, dtype=f) * f(2.0) / f(DH))).astype(f)
    angle = (np.arange(T, dtype=f)[:, None] * freq[None, :]).astype(f)
    cos, sin = np.cos(angle).astype(f), np.sin(angle).astype(f)
    heads = ROT // DH
    got["rope_in"] = np.stack([np.tile(np.concatenate([cos, cos], 1), (1, heads)),
                               np.tile(np.concatenate([-sin, sin], 1), (1, heads))], axis=1).astype(f)
    i, j = np.arange(T)[:, None], np.arange(T)[None, :]
    seen = [(i >= j) & ((j >= i - 64) | (j < 4)), i >= j]
    got["masks_in"] = np.stack([np.tile(np.where(s, 0.0, MASKED), (1, BLK)) for s in seen], axis=1)
    got["masks_in"] = bf16_bits(got["masks_in"])
    got["gate_in"] = np.concatenate([a["L0_ffn_gate_w"], a["L0_ffn_sgate_w"], np.zeros((1, D), f)]).T
    none = np.zeros((NC * 128 - HID, D), f)
    w13, shared = a["L0_ffn_w13"], a["L0_ffn_shared_gate_up_w"]
    g = np.concatenate([w13[:, :HE].reshape(-1, D), shared[:HS], none])
    u = np.concatenate([w13[:, HE:].reshape(-1, D), shared[HS:], none])
    d = np.concatenate([a["L0_ffn_w2"].transpose(0, 2, 1).reshape(-1, D), a["L0_ffn_shared_down_w"].T, none])
    gu = np.stack([g.reshape(NC, 128, KC, 128), u.reshape(NC, 128, KC, 128)], axis=1)
    gu = gu.transpose(0, 4, 3, 1, 2).reshape(NC, 128, KC * 256)
    got["chunks_in"] = np.concatenate([gu, d.reshape(NC, 128, D)], axis=2)
    owner = np.minimum(np.arange(NC * 128) // HE, NE)
    one = (owner.reshape(NC, 1, 128) == np.arange(NCO)[None, :, None])
    got["select_in"] = bf16_bits(np.tile(one, (1, PARTS, 1)))
    got["ident_in"] = np.eye(128, dtype=f)
    got["iota_in"] = np.arange(NE, dtype=f)
    return {k: np.ascontiguousarray(v) for k, v in got.items()}


def kernel(**inputs):
    import concourse.bacc as bacc
    from concourse.bass_utils import run_bass_kernel_spmd

    arrays = lay_out(inputs)
    nc = bacc.Bacc("TRN2", target_bir_lowering=False, num_devices=1)
    args = {k: nc.dram_tensor(f"{k}_dram", v.shape, mybir.dt.from_np(v.dtype), kind="ExternalInput").ap()
            for k, v in arrays.items()}
    out = nc.dram_tensor("out_dram", (B, T, D), F32, kind="ExternalOutput").ap()
    decoder_layer(nc, out=out, **args)
    r = run_bass_kernel_spmd(nc, [{f"{k}_dram": v for k, v in arrays.items()}], core_ids=[0])
    return r.results[0]["out_dram"]
```

```python
from contextlib import ExitStack

import numpy as np

import concourse.bass as bass
from concourse import mybir

F32 = mybir.dt.float32
F32R = mybir.dt.float32r
BF16 = mybir.dt.bfloat16
U32 = mybir.dt.uint32
U16 = mybir.dt.uint16
ALU = mybir.AluOpType
ACT = mybir.ActivationFunctionType
AX = mybir.AxisListType

B, T, D = 8, 128, 256
NH, DH, NG = 16, 16, 4
PAD = 32
BLK = 4
ROWT = 4
KC = D // 128
QKV = NH * DH + 2 * NG * DH
ROT = NH * DH + NG * DH
TOPK = 4
NE, HE, HS = 16, 176, 704
HID = NE * HE + HS
NC = -(-HID // 128)
RING = 4
PARTS = 3
NCO = NE + 1
HALF = 512
NHALF = B * T // HALF
WROW = KC * 256 + D
SCALE = DH ** -0.5
EPS = 1e-5
MASKED = -1e30


def decoder_layer(nc, x_in, ctx_in, wqkv_in, bqkv_in, wo_in, bo_in, rope_in, masks_in, gate_in,
                  chunks_in, select_in, ident_in, iota_in, out):
    ctx = ExitStack()
    with ctx:
        def sb(name, shape, dt=F32):
            return ctx.enter_context(nc.sbuf_tensor(name, shape, dt))

        def bank(name, dt=F32):
            return ctx.enter_context(nc.psum_tensor(name, [128, 2048 // mybir.dt.size(dt)], dt))

        def sem(name):
            return ctx.enter_context(nc.semaphore(name))

        ident = sb("ident", [128, 128])
        ident_b = sb("ident_b", [128, 128], BF16)
        masks = sb("masks", [128, 2, BLK * 128], BF16)
        rope = sb("rope", [128, 2, ROT])
        wqkv = sb("wqkv", [128, KC, QKV])
        bqkv = sb("bqkv", [128, QKV])
        wo = sb("wo", [128, KC, D])
        bo = sb("bo", [128, D])
        gate = sb("gate", [128, KC, NCO + 1])
        gate_h = sb("gate_h", [128, KC, NCO + 1], F32R)
        gate_l = sb("gate_l", [128, KC, NCO + 1], F32R)
        iota = sb("iota", [128, NE])
        expo = sb("expo", [128, B])
        zero_b = sb("zero_b", [1, HALF], BF16)

        x = sb("x", [128, B + 1, D])
        ctx_sb = sb("ctx_sb", [128, B, D])
        x2 = sb("x2", [128, B, D])
        x3 = sb("x3", [128, B, D])
        stat1 = sb("stat1", [128, B, 6])
        mv1 = sb("mv1", [128, B + 1, 2])
        ve1 = sb("ve1", [128, B])
        rstd1 = sb("rstd1", [128, B + 1])
        xth = sb("xth", [128, KC, B * T], F32R)
        xtl = sb("xtl", [128, KC, B * T], F32R)

        xn1 = sb("xn1", [128, D])
        xt1 = sb("xt1", [128, KC, 128])
        qkv = sb("qkv", [128, QKV])
        turned = sb("turned", [128, ROT])
        swapped = sb("swapped", [128, ROT])
        q_pad = sb("q_pad", [128, BLK, ROWT, PAD])
        k_pad = sb("k_pad", [128, NG, PAD])
        v_pad = sb("v_pad", [128, NG, PAD])
        qt = sb("qt", [128, BLK, 128])
        kt = sb("kt", [128, 128])
        qc_pad = sb("qc_pad", [128, BLK, ROWT, PAD])
        c_pad = sb("c_pad", [128, BLK, ROWT, PAD])
        qtc = sb("qtc", [128, BLK, 128])
        ktc = sb("ktc", [128, BLK, 128])
        neg_max = sb("neg_max", [128, ROWT, BLK])
        probs = sb("probs", [128, ROWT, BLK, 128])
        probs_t = sb("probs_t", [128, ROWT, BLK, 128])
        values_t = sb("values_t", [128, BLK, 128])
        inv = sb("inv", [128, NH])
        attn = sb("attn", [128, D])
        attn_t = sb("attn_t", [128, KC, 128])
        values_tc = sb("values_tc", [128, BLK, 128])
        inv_c = sb("inv_c", [128, NH])
        attn_c = sb("attn_c", [128, D])
        stat2 = sb("stat2", [128, 2, 6])
        mv2 = sb("mv2", [128, 2, 2])
        ve2 = sb("ve2", [128, 2])
        rstd2 = sb("rstd2", [128, 2])
        xn3 = sb("xn3", [128, D])
        spare = sb("spare", [128, 4])

        logits_t = sb("logits_t", [NCO + 1, B * T])
        logits = sb("logits", [128, B, NCO])
        top_l = sb("top_l", [128, B])
        ex = sb("ex", [128, B, NE])
        ex_g = sb("ex_g", [128, B])
        ex_g1 = sb("ex_g1", [128, B])
        ex_sum = sb("ex_sum", [128, B])
        ex_inv = sb("ex_inv", [128, B])
        top_v = sb("top_v", [128, B, 8])
        top_i = sb("top_i", [128, B, 8], U32)
        top_f = sb("top_f", [128, B, 8])
        picked = sb("picked", [128, TOPK, B, NE])
        coef = sb("coef", [128, B, NCO])
        coef_r = sb("coef_r", [128, 2, B, NCO])
        coef_b = sb("coef_b", [128, B, PARTS, NCO], BF16)
        coef_t = sb("coef_t", [PARTS * NCO, B * T], BF16)

        w_raw = sb("w_raw", [128, RING, WROW])
        w_h = sb("w_h", [128, RING, WROW], F32R)
        w_l = sb("w_l", [128, RING, WROW], F32R)
        sel = sb("sel", [PARTS * NCO, RING, 128], BF16)
        silu = sb("silu", [128, 2, HALF])
        gu = sb("gu", [128, 2, HALF])
        hid = sb("hid", [128, 2, HALF])
        hid_h = sb("hid_h", [128, 2, HALF], F32R)
        hid_l = sb("hid_l", [128, 2, HALF], F32R)
        y_t = sb("y_t", [128, KC, HALF])
        y = sb("y", [128, NHALF * 2, 2, D])

        pb = [bank(f"bank{i}") for i in range(8)]
        ps_s = [pb[g][:, :] for g in range(ROWT)]
        ps_x, ps_q, ps_o, ps_w = pb[4], pb[5], pb[6], pb[7]
        ps_g, ps_u, ps_c, ps_y, ps_t = [pb[0], pb[1]], [pb[2], pb[3]], pb[4], [pb[5], pb[6]], pb[7]

        x_first = sem("x_first")
        x_rest = sem("x_rest")
        ctx_loaded = sem("ctx_loaded")
        ident_loaded = sem("ident_loaded")
        wqkv_loaded = sem("wqkv_loaded")
        rope_loaded = sem("rope_loaded")
        masks_loaded = sem("masks_loaded")
        wo_loaded = sem("wo_loaded")
        gate_loaded = sem("gate_loaded")
        pads_ready = sem("pads_ready")
        ident_b_ready = sem("ident_b_ready")
        gate_h_ready = sem("gate_h_ready")
        gate_l_ready = sem("gate_l_ready")
        stats1_ready = sem("stats1_ready")
        var1_ready = sem("var1_ready")
        rstd1_ready = sem("rstd1_ready")
        xb_ready = sem("xb_ready")
        chain1 = sem("chain1")
        xn1_ready = sem("xn1_ready")
        xt1_psum = sem("xt1_psum")
        xt1_ready = sem("xt1_ready")
        qkv_psum = sem("qkv_psum")
        qkv_ready = sem("qkv_ready")
        rope_step = sem("rope_step")
        v_ready = sem("v_ready")
        qk_ready = sem("qk_ready")
        qkt_psum = sem("qkt_psum")
        qt_ready = sem("qt_ready")
        kt_ready = sem("kt_ready")
        scores_psum = [sem("scores_psum_s"), sem("scores_psum_c")]
        max_ready = [sem("max_ready_s"), sem("max_ready_c")]
        probs_ready = [sem("probs_ready_s"), sem("probs_ready_c")]
        probs_t_psum = [sem("probs_t_psum_s"), sem("probs_t_psum_c")]
        probs_t_ready = [[sem("probs_t_ready_s0"), sem("probs_t_ready_s1")],
                         [sem("probs_t_ready_c0"), sem("probs_t_ready_c1")]]
        values_psum = [sem("values_psum_s"), sem("values_psum_c")]
        values_taken = [sem("values_taken_s"), sem("values_taken_c")]
        rows_psum = [sem("rows_psum_s"), sem("rows_psum_c")]
        inv_ready = [sem("inv_ready_s"), sem("inv_ready_c")]
        attn_ready = [sem("attn_ready_s"), sem("attn_ready_c")]
        attn_t_psum = sem("attn_t_psum")
        attn_t_ready = sem("attn_t_ready")
        wo_psum = sem("wo_psum")
        x2_ready = sem("x2_ready")
        stat_ready = [sem("stat_ready_s"), sem("stat_ready_c")]
        mv_ready = [sem("mv_ready_s"), sem("mv_ready_c")]
        ve_ready = [sem("ve_ready_s"), sem("ve_ready_c")]
        rstd_ready = [sem("rstd_ready_s"), sem("rstd_ready_c")]
        xn2_ready = sem("xn2_ready")
        c_pad_ready = sem("c_pad_ready")
        ct_psum = sem("ct_psum")
        ktc_ready = sem("ktc_ready")
        qc_psum = sem("qc_psum")
        qtc_ready = sem("qtc_ready")
        x3_ready = sem("x3_ready")
        xn3_ready = sem("xn3_ready")
        xt3_psum = sem("xt3_psum")
        xth_ready = sem("xth_ready")
        xtl_ready = sem("xtl_ready")
        lt_psum = sem("lt_psum")
        lt_ready = sem("lt_ready")
        logits_psum = sem("logits_psum")
        route = sem("route")
        shifted_ready = sem("shifted_ready")
        exps_ready = sem("exps_ready")
        coef_ready = sem("coef_ready")
        coef_psum = sem("coef_psum")
        coef_t_ready = sem("coef_t_ready")
        w_loaded = [sem(f"w_loaded{r}") for r in range(RING)]
        wh_ready = sem("wh_ready")
        wl_ready = sem("wl_ready")
        up_psum = sem("up_psum")
        co_psum = sem("co_psum")
        silu_ready = sem("silu_ready")
        gu_ready = sem("gu_ready")
        hid_ready = sem("hid_ready")
        hidh_ready = sem("hidh_ready")
        hidl_ready = sem("hidl_ready")
        down_done = sem("down_done")
        yt_ready = sem("yt_ready")
        y_psum = sem("y_psum")
        y_ready = sem("y_ready")
        y_stored = sem("y_stored")

        block = ctx.enter_context(nc.Block())
        SELF, CROSS = 0, 1

        def store(sp, half, pair):
            m = 2 * half + pair
            sp.wait_ge(y_ready, m + 1)
            b = m * 2
            sp.dma_start(out[b:b + 2].rearrange("b p d -> p b d"), y[:, m, :, :]).then_inc(y_stored, 16)

        @block.sync
        def _(sp):
            sp.dma_start(x[:, 0, :], x_in[0]).then_inc(x_first, 16)
            sp.dma_start(ident[:, :], ident_in).then_inc(ident_loaded, 16)
            sp.dma_start(wqkv[:, :, :], wqkv_in.rearrange("(k p) n -> p k n", p=128)).then_inc(wqkv_loaded, 16)
            sp.dma_start(bqkv[:, :], bqkv_in.partition_broadcast(128)).then_inc(rope_loaded, 16)
            sp.dma_start(rope[:, :, :], rope_in).then_inc(rope_loaded, 16)
            sp.dma_start(masks[:, :, :].bitcast(U16), masks_in).then_inc(masks_loaded, 16)
            sp.dma_start(x[:, 1:B, :], x_in[1:B].rearrange("b p d -> p b d")).then_inc(x_rest, 16)
            sp.dma_start(bo[:, :], bo_in.partition_broadcast(128)).then_inc(wo_loaded, 16)
            sp.dma_start(wo[:, :, :], wo_in.rearrange("(k p) n -> p k n", p=128)).then_inc(wo_loaded, 16)
            sp.dma_start(ctx_sb[:, :, :], ctx_in.rearrange("b p d -> p b d")).then_inc(ctx_loaded, 16)
            sp.dma_start(gate[:, :, :], gate_in.rearrange("(k p) n -> p k n", p=128)).then_inc(gate_loaded, 16)
            sp.dma_start(iota[:, :], iota_in.partition_broadcast(128)).then_inc(gate_loaded, 16)

            def load_chunk(n, c, r):
                if not isinstance(n, int) or n >= RING:
                    sp.wait_ge(wl_ready, n - RING + 1)
                    sp.wait_ge(co_psum, n - RING + 1)
                sp.dma_start(w_raw[:, r, :], chunks_in[bass.ds(c, 1)].rearrange("c p n -> p (c n)")).then_inc(w_loaded[r], 16)
                sp.dma_start(sel[:, r, :].bitcast(U16), select_in[bass.ds(c, 1)].rearrange("c p n -> p (c n)")).then_inc(w_loaded[r], 16)

            for half in range(NHALF):
                for r in range(RING):
                    load_chunk(half * NC + r, r, r)
                if half:
                    for pair in range(2):
                        store(sp, half - 1, pair)
                with sp.Fori(1, NC // RING) as turn:
                    for r in range(RING):
                        load_chunk(turn * RING + (half * NC + r), turn * RING + r, r)
            for pair in range(2):
                store(sp, 1, pair)
            sp.wait_ge(y_stored, 16 * NHALF * 2)

        @block.gpsimd
        def _(pool):
            pool.memset(q_pad[:, :, :, :], 0.0).then_inc(pads_ready, 1)
            pool.memset(k_pad[:, :, :], 0.0).then_inc(pads_ready, 1)
            pool.memset(v_pad[:, :, :], 1.0).then_inc(pads_ready, 1)
            pool.memset(expo[:, :], -0.5).then_inc(pads_ready, 1)
            pool.memset(rstd1[:, B:B + 1], 0.0).then_inc(pads_ready, 1)
            pool.memset(mv1[:, B:B + 1, :], 0.0).then_inc(pads_ready, 1)
            pool.memset(qc_pad[:, :, :, :], 0.0).then_inc(pads_ready, 1)
            pool.memset(c_pad[:, :, :, :], 1.0).then_inc(pads_ready, 1)
            pool.memset(zero_b[:, :], 0.0).then_inc(pads_ready, 1)
            pool.memset(x[:, B, :], 0.0).then_inc(pads_ready, 1)
            pool.wait_ge(ident_loaded, 16)
            pool.tensor_copy(ident_b[:, :], ident[:, :]).then_inc(ident_b_ready, 1)
            pool.wait_ge(pads_ready, 10)
            pool.wait_ge(var1_ready, 1)
            pool.tensor_tensor(rstd1[:, 0:1], ve1[:, 0:1], expo[:, 0:1], ALU.pow).then_inc(rstd1_ready, 1)
            pool.wait_ge(var1_ready, 2)
            pool.tensor_tensor(rstd1[:, 1:B], ve1[:, 1:B], expo[:, 1:B], ALU.pow).then_inc(rstd1_ready, 1)
            pool.wait_ge(x_first, 16)
            pool.wait_ge(x_rest, 16)
            pool.wait_ge(wo_loaded, 32)
            for b in range(B):
                ins = pool.tensor_tensor(x2[:, b, :], x[:, b, :], bo[:, :], ALU.add)
            ins.then_inc(xb_ready, 1)
            pool.wait_ge(ctx_loaded, 16)

            def inverse_deviation(kind, b):
                pool.wait_ge(ve_ready[kind], b + 1)
                pool.tensor_tensor(rstd2[:, kind:kind + 1], ve2[:, kind:kind + 1], expo[:, 0:1], ALU.pow
                                   ).then_inc(rstd_ready[kind], 1)

            def iteration(t, self_on, cross_on, tail_on):
                if cross_on:
                    if tail_on:
                        pool.wait_ge(values_psum[CROSS], 2 * (t - 1))
                    pool.tensor_copy(c_pad[:, :, :, 0:DH],
                                     ctx_sb[:, bass.ds(t - 1, 1), :].rearrange("p b (j g d) -> p (b j) g d", j=BLK, g=ROWT)
                                     ).then_inc(c_pad_ready, 1)
                if tail_on:
                    inverse_deviation(CROSS, t - 2)
                if self_on:
                    inverse_deviation(SELF, t)

            iteration(0, True, False, False)
            iteration(1, True, True, False)
            with pool.Fori(2, B) as t:
                iteration(t, True, True, True)
            iteration(B, False, True, True)
            inverse_deviation(CROSS, B - 1)

            def low_part(n, r):
                pool.wait_ge(wh_ready, n + 1)
                pool.tensor_tensor(w_l[:, r, :], w_raw[:, r, :], w_h[:, r, :].bitcast(F32), ALU.subtract
                                   ).then_inc(wl_ready, 1)

            with pool.Fori(0, NHALF * NC, RING) as n:
                for r in range(RING):
                    low_part(n + r, r)

        @block.scalar
        def _(act):
            def front_a(f):
                act.wait_ge(xt1_psum, f + 1)
                act.activation(xt1[:, :, :], ps_w[:, 0:KC * 128].rearrange("p (k n) -> p k n", k=KC), ACT.Copy
                               ).then_inc(xt1_ready, 1)

            def front_c(f):
                act.wait_ge(qkt_psum, f + 1)
                act.activation(qt[:, :, :], ps_q[:, :].rearrange("p (j n) -> p j n", j=BLK), ACT.Copy, scale=SCALE
                               ).then_inc(qt_ready, 1)

            def cross_q(c):
                act.wait_ge(qc_psum, c + 1)
                act.activation(qtc[:, :, :], ps_q[:, :].rearrange("p (j n) -> p j n", j=BLK), ACT.Copy, scale=SCALE
                               ).then_inc(qtc_ready, 1)

            def exps(kind, b, u):
                for g in (2 * u, 2 * u + 1):
                    act.wait_ge(max_ready[kind], 4 * b + g + 1)
                    for j in range(BLK):
                        ins = act.activation(probs[:, g, j, :], ps_s[g][:, 128 * j:128 * j + 128], ACT.Exp,
                                             bias=neg_max[:, g, j:j + 1])
                    ins.then_inc(probs_ready[kind], 1)

            def take_probs_t(kind, b, g):
                act.wait_ge(probs_t_psum[kind], 4 * b + g + 1)
                act.activation(probs_t[:, g, :, :], ps_s[g].rearrange("p (j n) -> p j n", j=BLK), ACT.Copy
                               ).then_inc(probs_t_ready[kind][g // 2], 1)

            def take_values(b):
                act.wait_ge(values_psum[CROSS], 2 * b + 2)
                act.activation(values_tc[:, :, :], ps_o[:, :].rearrange("p (j n) -> p j n", j=BLK), ACT.Copy
                               ).then_inc(values_taken[CROSS], 1)

            def take_attn_t(b):
                act.wait_ge(attn_t_psum, b + 1)
                act.activation(attn_t[:, :, :], ps_x[:, 0:KC * 128].rearrange("p (k n) -> p k n", k=KC), ACT.Copy
                               ).then_inc(attn_t_ready, 1)

            def take_xth(b):
                act.wait_ge(xt3_psum, b + 1)
                act.activation(xth[:, :, bass.ds(b * T, T)],
                               ps_x[:, 0:KC * 128].rearrange("p (k n) -> p k n", k=KC), ACT.Copy
                               ).then_inc(xth_ready, 1)

            def iteration(t, self_on, cross_on, tail_on):
                if tail_on:
                    take_values(t - 2)
                if self_on:
                    exps(SELF, t, 0)
                    front_a(t + 1)
                    exps(SELF, t, 1)
                if cross_on:
                    cross_q(t - 1)
                if self_on:
                    take_probs_t(SELF, t, 2)
                if tail_on:
                    take_xth(t - 2)
                if cross_on:
                    exps(CROSS, t - 1, 0)
                    exps(CROSS, t - 1, 1)
                if self_on:
                    front_c(t + 1)
                if cross_on:
                    take_probs_t(CROSS, t - 1, 2)
                if self_on:
                    take_attn_t(t)

            front_a(0)
            front_c(0)
            iteration(0, True, False, False)
            iteration(1, True, True, False)
            with act.Fori(2, B) as t:
                iteration(t, True, True, True)
            iteration(B, False, True, True)
            take_values(B - 1)
            take_xth(B - 1)

            def high_part(n, r, m):
                act.wait_ge(w_loaded[r], 32 * (m + 1))
                if not isinstance(n, int) or n >= RING:
                    act.wait_ge(down_done, n - RING + 1)
                act.activation(w_h[:, r, :], w_raw[:, r, :], ACT.Copy).then_inc(wh_ready, 1)

            high_part(0, 0, 0)
            high_part(1, 1, 0)

            act.wait_ge(lt_psum, 1)
            act.activation(logits_t[:, 0:HALF], pb[0][0:NCO + 1, :], ACT.Copy).then_inc(lt_ready, 1)
            act.wait_ge(lt_psum, 2)
            act.activation(logits_t[:, HALF:], pb[1][0:NCO + 1, :], ACT.Copy).then_inc(lt_ready, 1)
            act.wait_ge(shifted_ready, 1)
            act.activation(ex[:, :, :], ex[:, :, :], ACT.Exp).then_inc(exps_ready, 1)
            act.activation(ex_g[:, :], logits[:, :, NE], ACT.Exp, scale=-1.0).then_inc(exps_ready, 1)
            act.wait_ge(coef_psum, 1)
            act.activation(coef_t[:, :], pb[3][0:PARTS * NCO, :].bitcast(BF16), ACT.Copy).then_inc(coef_t_ready, 1)

            def chunk(n, k, q, ahead=True):
                if ahead:
                    r = (k + 2) % RING
                    high_part(n + 2, r, q + (k + 2) // RING)
                act.wait_ge(up_psum, 2 * n + 1)
                if not isinstance(n, int) or n >= 2:
                    act.wait_ge(gu_ready, n - 1)
                act.activation(silu[:, k % 2, :], ps_g[k % 2][:, :], ACT.Silu).then_inc(silu_ready, 1)
                act.wait_ge(hid_ready, n + 1)
                if not isinstance(n, int) or n >= 2:
                    act.wait_ge(down_done, n - 1)
                act.activation(hid_h[:, k % 2, :], hid[:, k % 2, :], ACT.Copy).then_inc(hidh_ready, 1)

            turns = NC // RING
            for half in range(NHALF):
                if half == 0:
                    for k in range(RING):
                        chunk(k, k, 0)
                    first = 1
                else:
                    first = 0
                with act.Fori(first, turns - 1) as i:
                    q = half * turns + i
                    for k in range(RING):
                        chunk(q * RING + k, k, q)
                q = half * turns + turns - 1
                for k in range(RING):
                    chunk(q * RING + k, k, q, ahead=half == 0 or k < RING - 2)
                act.wait_ge(down_done, (half + 1) * NC)
                act.activation(y_t[:, 0, :], ps_y[0][:, :], ACT.Copy).then_inc(yt_ready, 1)

        @block.vector
        def _(dve):
            def one(ap, i):
                return ap[:, bass.ds(i, 1), :].rearrange("p b d -> p (b d)")

            links = [0]

            def link(ins):
                links[0] += 1
                ins.then_inc(chain1, 1)
                dve.wait_ge(chain1, links[0])

            dve.wait_ge(x_first, 16)
            link(dve.bn_stats(stat1[:, 0, :], x[:, 0, :]))
            dve.wait_ge(pads_ready, 10)
            link(dve.bn_aggr(mv1[:, 0, :], stat1[:, 0, :]))
            dve.tensor_scalar(ve1[:, 0:1], mv1[:, 0, 1:2], EPS, None, ALU.add).then_inc(var1_ready, 1)
            dve.wait_ge(x_rest, 16)
            for b in range(1, B):
                dve.bn_stats(stat1[:, b, :], x[:, b, :]).then_inc(stats1_ready, 1)
            for b in range(1, B):
                dve.wait_ge(stats1_ready, b)
                dve.bn_aggr(mv1[:, b, :], stat1[:, b, :]).then_inc(stats1_ready, 1)
            dve.wait_ge(stats1_ready, 2 * (B - 1))
            dve.tensor_scalar(ve1[:, 1:B], mv1[:, 1:B, 1], EPS, None, ALU.add).then_inc(var1_ready, 1)

            def front_n(f):
                dve.wait_ge(xt1_psum, f)
                dve.tensor_scalar(xn1[:, :], one(x, f), mv1[:, bass.ds(f, 1), 0], rstd1[:, bass.ds(f, 1)], ALU.subtract, ALU.mult).then_inc(xn1_ready, 1)

            def front_r(f):
                dve.wait_ge(qkv_psum, f + 1)
                dve.tensor_tensor(qkv[:, :], ps_w[:, 0:QKV], bqkv[:, :], ALU.add).then_inc(qkv_ready, 1)
                dve.wait_ge(qkv_ready, f + 1)
                halves = qkv[:, 0:ROT].rearrange("p (h s i) -> p h s i", s=2, i=DH // 2)
                sines = rope[:, 1, :].rearrange("p (h s i) -> p h s i", s=2, i=DH // 2)
                turn = swapped[:, :].rearrange("p (h s i) -> p h s i", s=2, i=DH // 2)
                dve.tensor_tensor(turned[:, :], qkv[:, 0:ROT], rope[:, 0, :], ALU.mult).then_inc(rope_step, 1)
                dve.tensor_tensor(turn[:, :, 0, :], halves[:, :, 1, :], sines[:, :, 0, :], ALU.mult).then_inc(rope_step, 1)
                dve.tensor_tensor(turn[:, :, 1, :], halves[:, :, 0, :], sines[:, :, 1, :], ALU.mult).then_inc(rope_step, 1)

            def front_p(f):
                dve.wait_ge(rope_step, 3 * (f + 1))
                nq = NH * DH
                dve.tensor_tensor(q_pad[:, :, :, 0:DH].rearrange("p j g d -> p g j d"),
                                  turned[:, 0:nq].rearrange("p (g j d) -> p g j d", g=NG, j=BLK),
                                  swapped[:, 0:nq].rearrange("p (g j d) -> p g j d", g=NG, j=BLK), ALU.add
                                  ).then_inc(qk_ready, 1)
                dve.tensor_tensor(k_pad[:, :, 0:DH],
                                  turned[:, nq:ROT].rearrange("p (g d) -> p g d", g=NG),
                                  swapped[:, nq:ROT].rearrange("p (g d) -> p g d", g=NG), ALU.add).then_inc(qk_ready, 1)

            def front_v(f):
                if not isinstance(f, int) or f:
                    dve.wait_ge(values_psum[SELF], 2 * f)
                dve.tensor_copy(v_pad[:, :, 0:DH], qkv[:, ROT:QKV].rearrange("p (g d) -> p g d", g=NG)
                                ).then_inc(v_ready, 1)

            def front_k(f):
                dve.wait_ge(qkt_psum, f + 1)
                dve.tensor_copy(kt[:, :], ps_w[:, 0:128]).then_inc(kt_ready, 1)

            def row_max(kind, b, u):
                for g in (2 * u, 2 * u + 1):
                    dve.wait_ge(scores_psum[kind], 4 * b + g + 1)
                    dve.tensor_reduce(neg_max[:, g, :], ps_s[g].rearrange("p (j n) -> p j n", j=BLK), AX.X, ALU.max,
                                      negate=True).then_inc(max_ready[kind], 1)

            def take_probs_t(kind, b, g):
                dve.wait_ge(probs_t_psum[kind], 4 * b + g + 1)
                dve.tensor_copy(probs_t[:, g, :, :], ps_s[g].rearrange("p (j n) -> p j n", j=BLK)
                                ).then_inc(probs_t_ready[kind][g // 2], 1)

            def take_values(b):
                dve.wait_ge(values_psum[SELF], 2 * b + 2)
                dve.tensor_copy(values_t[:, :, :], ps_o[:, :].rearrange("p (j n) -> p j n", j=BLK)
                                ).then_inc(values_taken[SELF], 1)

            def normalise(kind, b, inverse, result):
                dve.wait_ge(rows_psum[kind], b + 1)
                heads = ps_o[:, :].rearrange("p (h c) -> p h c", h=NH)
                dve.reciprocal(inverse[:, :], heads[:, :, DH]).then_inc(inv_ready[kind], 1)
                dve.wait_ge(inv_ready[kind], b + 1)
                if kind == SELF:
                    heads = heads.rearrange("p (j g) c -> p j g c", j=BLK)
                    dve.tensor_tensor(result[:, :].rearrange("p (g j d) -> p j g d", g=NG, j=BLK), heads[:, :, :, 0:DH],
                                      inverse[:, :].rearrange("p (j g) -> p j g", j=BLK).unsqueeze(3).broadcast_to([128, BLK, NG, DH]),
                                      ALU.mult).then_inc(attn_ready[kind], 1)
                else:
                    dve.tensor_tensor(result[:, :].rearrange("p (h d) -> p h d", h=NH), heads[:, :, 0:DH],
                                      inverse[:, :].unsqueeze(2).broadcast_to([128, NH, DH]), ALU.mult
                                      ).then_inc(attn_ready[kind], 1)

            def carry_wait(i):
                dve.memset(spare[:, i:i + 1], 0.0)

            def statistics(kind, b):
                rows, rows_ready = ((x2, x2_ready), (x3, x3_ready))[kind]
                dve.wait_ge(rows_ready, b + 1)
                carry_wait(2 * kind)
                dve.bn_stats(stat2[:, kind, :], one(rows, b)).then_inc(stat_ready[kind], 1)
                dve.wait_ge(stat_ready[kind], b + 1)
                carry_wait(2 * kind + 1)
                dve.bn_aggr(mv2[:, kind, :], stat2[:, kind, :]).then_inc(mv_ready[kind], 1)
                dve.wait_ge(mv_ready[kind], b + 1)
                dve.tensor_scalar(ve2[:, kind:kind + 1], mv2[:, kind, 1:2], EPS, None, ALU.add
                                  ).then_inc(ve_ready[kind], 1)

            def cross_rows(b):
                normalise(CROSS, b, inv_c, attn_c)
                dve.wait_ge(attn_ready[CROSS], b + 1)
                dve.tensor_tensor(one(x3, b), attn_c[:, :], one(x2, b), ALU.add).then_inc(x3_ready, 1)

            def third_norm(b):
                dve.wait_ge(rstd_ready[CROSS], b + 1)
                dve.tensor_scalar(xn3[:, :], one(x3, b), mv2[:, CROSS, 0:1], rstd2[:, CROSS:CROSS + 1],
                                  ALU.subtract, ALU.mult).then_inc(xn3_ready, 1)

            def take_xtl(b):
                dve.wait_ge(xth_ready, b + 1)
                cols = bass.ds(b * T, T)
                dve.tensor_tensor(xtl[:, :, cols], ps_x[:, 0:KC * 128].rearrange("p (k n) -> p k n", k=KC),
                                  xth[:, :, cols].bitcast(F32), ALU.subtract).then_inc(xtl_ready, 1)

            def iteration(t, self_on, cross_on, tail_on):
                if self_on:
                    front_n(t + 1)
                    row_max(SELF, t, 0)
                if tail_on:
                    cross_rows(t - 2)
                if self_on:
                    row_max(SELF, t, 1)
                if cross_on:
                    dve.wait_ge(ct_psum, t)
                    dve.tensor_copy(ktc[:, :, :], ps_x[:, :].rearrange("p (j n) -> p j n", j=BLK)).then_inc(ktc_ready, 1)
                if tail_on:
                    statistics(CROSS, t - 2)
                if self_on:
                    take_probs_t(SELF, t, 0)
                    take_probs_t(SELF, t, 1)
                if tail_on:
                    third_norm(t - 2)
                if self_on:
                    take_probs_t(SELF, t, 3)
                    front_r(t + 1)
                if cross_on:
                    row_max(CROSS, t - 1, 0)
                if tail_on:
                    take_xtl(t - 2)
                if self_on:
                    front_p(t + 1)
                if cross_on:
                    row_max(CROSS, t - 1, 1)
                if self_on:
                    take_values(t)
                if cross_on:
                    take_probs_t(CROSS, t - 1, 0)
                    take_probs_t(CROSS, t - 1, 1)
                if self_on:
                    normalise(SELF, t, inv, attn)
                    front_k(t + 1)
                    front_v(t + 1)
                if cross_on:
                    take_probs_t(CROSS, t - 1, 3)
                if self_on:
                    dve.wait_ge(wo_psum, t + 1)
                    if isinstance(t, int):
                        dve.wait_ge(xb_ready, 1)
                    dve.tensor_tensor(one(x2, t), ps_w[:, 0:D], one(x2, t), ALU.add).then_inc(x2_ready, 1)
                    statistics(SELF, t)
                    dve.wait_ge(rstd_ready[SELF], t + 1)
                    dve.tensor_scalar(qc_pad[:, :, :, 0:DH],
                                      one(x2, t).rearrange("p (j g d) -> p j g d", j=BLK, g=ROWT),
                                      mv2[:, SELF, 0:1], rstd2[:, SELF:SELF + 1], ALU.subtract, ALU.mult
                                      ).then_inc(xn2_ready, 1)

            dve.wait_ge(rstd1_ready, 1)
            front_n(0)
            dve.wait_ge(rope_loaded, 32)
            front_r(0)
            front_p(0)
            front_v(0)
            front_k(0)
            dve.wait_ge(rstd1_ready, 2)
            iteration(0, True, False, False)
            iteration(1, True, True, False)
            with dve.Fori(2, B) as t:
                iteration(t, True, True, True)
            iteration(B, False, True, True)
            cross_rows(B - 1)
            statistics(CROSS, B - 1)
            third_norm(B - 1)
            dve.wait_ge(gate_loaded, 32)
            dve.tensor_copy(gate_h[:, :, :], gate[:, :, :]).then_inc(gate_h_ready, 1)
            dve.wait_ge(gate_h_ready, 1)
            dve.tensor_tensor(gate_l[:, :, :], gate[:, :, :], gate_h[:, :, :].bitcast(F32), ALU.subtract
                              ).then_inc(gate_l_ready, 1)
            take_xtl(B - 1)

            def over(ap, n):
                return ap.unsqueeze(2).broadcast_to([128, B, n])

            dve.wait_ge(logits_psum, 1)
            link(dve.tensor_copy(logits[:, :, :],
                                 pb[2][:, 0:B * (NCO + 1)].rearrange("p (b e) -> p b e", b=B)[:, :, 0:NCO]))
            link(dve.tensor_reduce(top_l[:, :], logits[:, :, 0:NE], AX.X, ALU.max))
            dve.tensor_tensor(ex[:, :, :], logits[:, :, 0:NE], over(top_l[:, :], NE), ALU.subtract
                              ).then_inc(shifted_ready, 1)
            dve.wait_ge(exps_ready, 2)
            dve.tensor_scalar(ex_g1[:, :], ex_g[:, :], 1.0, None, ALU.add).then_inc(chain1, 1)
            dve.tensor_reduce(ex_sum[:, :], ex[:, :, :], AX.X, ALU.add).then_inc(chain1, 1)
            links[0] += 2
            for b in range(B):
                dve.max(top_v[:, b, :], ex[:, b, :]).then_inc(route, 1)
            for b in range(B):
                dve.wait_ge(route, b + 1)
                dve.max_index(top_i[:, b, :], top_v[:, b, :], ex[:, b, :]).then_inc(route, 1)
            dve.wait_ge(chain1, links[0])
            dve.reciprocal(ex_inv[:, :], ex_sum[:, :]).then_inc(chain1, 1)
            dve.reciprocal(coef[:, :, NE], ex_g1[:, :]).then_inc(chain1, 1)
            links[0] += 2
            dve.wait_ge(route, 2 * B)
            link(dve.tensor_copy(top_f[:, :, :], top_i[:, :, :]))
            for k in range(TOPK):
                dve.tensor_tensor(picked[:, k, :, :], iota[:, :].unsqueeze(1).broadcast_to([128, B, NE]), over(top_f[:, :, k], NE),
                                  ALU.is_equal).then_inc(chain1, 1)
                links[0] += 1
            dve.wait_ge(chain1, links[0])
            for k in range(TOPK):
                dve.tensor_tensor(picked[:, k, :, :], picked[:, k, :, :], over(top_v[:, :, k], NE), ALU.mult
                                  ).then_inc(chain1, 1)
                links[0] += 1
            dve.wait_ge(chain1, links[0])
            link(dve.tensor_tensor(picked[:, 0:2, :, :], picked[:, 0:2, :, :], picked[:, 2:4, :, :], ALU.add))
            link(dve.tensor_tensor(picked[:, 0, :, :], picked[:, 0, :, :], picked[:, 1, :, :], ALU.add))
            link(dve.tensor_tensor(coef[:, :, 0:NE], picked[:, 0, :, :], over(ex_inv[:, :], NE), ALU.mult))
            link(dve.tensor_copy(coef_b[:, :, 0, :], coef[:, :, :]))
            link(dve.tensor_tensor(coef_r[:, 0, :, :], coef[:, :, :], coef_b[:, :, 0, :], ALU.subtract))
            link(dve.tensor_copy(coef_b[:, :, 1, :], coef_r[:, 0, :, :]))
            link(dve.tensor_tensor(coef_r[:, 1, :, :], coef_r[:, 0, :, :], coef_b[:, :, 1, :], ALU.subtract))
            dve.tensor_copy(coef_b[:, :, 2, :], coef_r[:, 1, :, :]).then_inc(coef_ready, 1)

            def chunk(n, k):
                dve.wait_ge(silu_ready, n + 1)
                dve.wait_ge(up_psum, 2 * n + 2)
                dve.tensor_tensor(gu[:, k % 2, :], silu[:, k % 2, :], ps_u[k % 2][:, :], ALU.mult).then_inc(gu_ready, 1)
                dve.wait_ge(gu_ready, n + 1)
                dve.wait_ge(co_psum, n + 1)
                if not isinstance(n, int) or n >= 2:
                    dve.wait_ge(hidl_ready, n - 1)
                dve.tensor_tensor(hid[:, k % 2, :], gu[:, k % 2, :], ps_c[:, :], ALU.mult).then_inc(hid_ready, 1)
                dve.wait_ge(hidh_ready, n + 1)
                dve.tensor_tensor(hid_l[:, k % 2, :], hid[:, k % 2, :], hid_h[:, k % 2, :].bitcast(F32), ALU.subtract
                                  ).then_inc(hidl_ready, 1)

            def finish(half):
                dve.wait_ge(down_done, (half + 1) * NC)
                dve.tensor_copy(y_t[:, 1, :], ps_y[1][:, :]).then_inc(yt_ready, 1)

            def sum_rows(half, pair):
                m = 2 * half + pair
                dve.wait_ge(y_psum, m + 1)
                dve.tensor_tensor(y[:, m, :, :], ps_t[:, :].rearrange("p (b d) -> p b d", b=2),
                                  x3[:, 2 * m:2 * m + 2, :], ALU.add).then_inc(y_ready, 1)

            for k in range(RING):
                chunk(k, k)
            with dve.Fori(RING, NC, RING) as n:
                for k in range(RING):
                    chunk(n + k, k)
            finish(0)
            for k in range(RING):
                chunk(NC + k, k)
                if k < 2:
                    sum_rows(0, k)
            with dve.Fori(NC + RING, 2 * NC, RING) as n:
                for k in range(RING):
                    chunk(n + k, k)
            finish(1)
            for pair in range(2):
                sum_rows(1, pair)

        @block.tensor
        def _(pe):
            def front_a(f):
                pe.wait_ge(xn1_ready, f + 1)
                if not isinstance(f, int) or f >= 2:
                    pe.wait_ge(x2_ready, f - 1)
                for k in range(KC):
                    ins = pe.transpose(ps_w[:, 128 * k:128 * k + 128], xn1[:, 128 * k:128 * k + 128], ident[:, :])
                ins.then_inc(xt1_psum, 1)

            def front_b(f):
                pe.wait_ge(xt1_ready, f + 1)
                for k in range(KC):
                    ins = pe.matmul(ps_w[:, 0:QKV], xt1[:, k, :], wqkv[:, k, :], start=k == 0, stop=k == KC - 1)
                ins.then_inc(qkv_psum, 1)

            def front_c(f):
                pe.wait_ge(qk_ready, 2 * f + 2)
                if not isinstance(f, int) or f >= 2:
                    pe.wait_ge(qtc_ready, f - 1)
                for j in range(BLK):
                    pe.transpose(ps_q[:, 128 * j:128 * j + 128], q_pad[:, j, :, :].rearrange("p g d -> p (g d)"),
                                 ident[:, :])
                pe.transpose(ps_w[:, 0:128], k_pad[:, :, :].rearrange("p g d -> p (g d)"), ident[:, :]
                             ).then_inc(qkt_psum, 1)

            def scores(kind, b, u):
                queries = qt if kind == SELF else qtc
                for g in (2 * u, 2 * u + 1):
                    pe.matmul(ps_s[g], ident_b[:, :], masks[:, kind, :], start=True, stop=False)
                for j in range(BLK):
                    for g in (2 * u, 2 * u + 1):
                        rows = slice(PAD * g, PAD * g + DH)
                        keys = kt[rows, :] if kind == SELF else ktc[rows, j, :]
                        ins = pe.matmul(ps_s[g][:, 128 * j:128 * j + 128], queries[rows, j, :], keys,
                                        start=False, stop=j == BLK - 1)
                        if j == BLK - 1:
                            ins.then_inc(scores_psum[kind], 1)

            def transpose_probs(kind, b, u):
                for g in (2 * u, 2 * u + 1):
                    pe.wait_ge(probs_ready[kind], 4 * b + g + 1)
                    for j in range(BLK):
                        ins = pe.transpose(ps_s[g][:, 128 * j:128 * j + 128], probs[:, g, j, :], ident[:, :])
                    ins.then_inc(probs_t_psum[kind], 1)

            def values(kind, b, u):
                pe.wait_ge(probs_t_ready[kind][u], 2 * b + 2)
                if kind == SELF:
                    pe.wait_ge(v_ready, b + 1)
                for g in (2 * u, 2 * u + 1):
                    out_rows = slice(PAD * g, PAD * g + PAD)
                    if kind == SELF:
                        ins = pe.matmul(ps_o[out_rows, :], v_pad[:, g, :],
                                        probs_t[:, g, :, :].rearrange("p j n -> p (j n)"), start=True, stop=True)
                        continue
                    for j in range(BLK):
                        ins = pe.matmul(ps_o[out_rows, 128 * j:128 * j + 128], c_pad[:, j, g, :], probs_t[:, g, j, :],
                                        start=True, stop=True)
                ins.then_inc(values_psum[kind], 1)

            def turn_values(kind, b):
                pe.wait_ge(values_taken[kind], b + 1)
                for j in range(BLK):
                    ins = pe.transpose(ps_o[:, 128 * j:128 * j + 128], (values_t if kind == SELF else values_tc)[:, j, :],
                                       ident[:, :])
                ins.then_inc(rows_psum[kind], 1)

            def turn_attn(b):
                pe.wait_ge(attn_ready[SELF], b + 1)
                for k in range(KC):
                    ins = pe.transpose(ps_x[:, 128 * k:128 * k + 128], attn[:, 128 * k:128 * k + 128], ident[:, :])
                ins.then_inc(attn_t_psum, 1)

            def project(b):
                pe.wait_ge(attn_t_ready, b + 1)
                pe.wait_ge(kt_ready, b + 2)
                for k in range(KC):
                    ins = pe.matmul(ps_w[:, 0:D], attn_t[:, k, :], wo[:, k, :], start=k == 0, stop=k == KC - 1)
                ins.then_inc(wo_psum, 1)

            def cross_keys(c):
                pe.wait_ge(c_pad_ready, c + 1)
                pe.wait_ge(attn_t_ready, c + 1)
                for j in range(BLK):
                    ins = pe.transpose(ps_x[:, 128 * j:128 * j + 128],
                                       c_pad[:, j, :, :].rearrange("p g d -> p (g d)"), ident[:, :])
                ins.then_inc(ct_psum, 1)

            def cross_queries(c):
                pe.wait_ge(xn2_ready, c + 1)
                pe.wait_ge(qt_ready, c + 2)
                for j in range(BLK):
                    ins = pe.transpose(ps_q[:, 128 * j:128 * j + 128],
                                       qc_pad[:, j, :, :].rearrange("p g d -> p (g d)"), ident[:, :])
                ins.then_inc(qc_psum, 1)

            def third_norm(b):
                pe.wait_ge(xn3_ready, b + 1)
                for k in range(KC):
                    ins = pe.transpose(ps_x[:, 128 * k:128 * k + 128], xn3[:, 128 * k:128 * k + 128], ident[:, :])
                ins.then_inc(xt3_psum, 1)

            def iteration(t, self_on, cross_on, tail_on):
                c = t - 1
                if self_on:
                    pe.wait_ge(qt_ready, t + 1)
                    pe.wait_ge(kt_ready, t + 1)
                    scores(SELF, t, 0)
                if tail_on:
                    turn_values(CROSS, t - 2)
                if self_on:
                    scores(SELF, t, 1)
                    front_a(t + 1)
                if cross_on:
                    cross_keys(c)
                    cross_queries(c)
                if self_on:
                    transpose_probs(SELF, t, 0)
                    front_b(t + 1)
                    transpose_probs(SELF, t, 1)
                if cross_on:
                    pe.wait_ge(qtc_ready, t)
                    pe.wait_ge(ktc_ready, t)
                    if self_on:
                        pe.wait_ge(probs_t_ready[SELF][0], 2 * t + 2)
                    scores(CROSS, c, 0)
                if self_on:
                    if tail_on:
                        pe.wait_ge(attn_ready[CROSS], t - 1)
                    values(SELF, t, 0)
                if tail_on:
                    third_norm(t - 2)
                if cross_on:
                    if self_on:
                        pe.wait_ge(probs_t_ready[SELF][1], 2 * t + 2)
                    scores(CROSS, c, 1)
                if self_on:
                    values(SELF, t, 1)
                if cross_on:
                    transpose_probs(CROSS, c, 0)
                if self_on:
                    front_c(t + 1)
                    turn_values(SELF, t)
                if cross_on:
                    transpose_probs(CROSS, c, 1)
                if self_on:
                    if tail_on:
                        pe.wait_ge(xtl_ready, t - 1)
                    elif cross_on:
                        pe.wait_ge(ktc_ready, t)
                    turn_attn(t)
                if cross_on:
                    if not self_on:
                        pe.wait_ge(attn_ready[CROSS], t - 1)
                    values(CROSS, c, 0)
                if self_on:
                    project(t)
                if cross_on:
                    values(CROSS, c, 1)

            pe.wait_ge(ident_loaded, 16)
            pe.wait_ge(pads_ready, 10)
            front_a(0)
            pe.wait_ge(wqkv_loaded, 16)
            front_b(0)
            front_c(0)
            pe.wait_ge(ident_b_ready, 1)
            pe.wait_ge(masks_loaded, 16)
            pe.wait_ge(wo_loaded, 32)
            iteration(0, True, False, False)
            iteration(1, True, True, False)
            with pe.Fori(2, B) as t:
                iteration(t, True, True, True)
            iteration(B, False, True, True)
            turn_values(CROSS, B - 1)
            third_norm(B - 1)

            def three(outs, pairs_h, pairs_l, first, last):
                n = len(pairs_h)
                todo = [(pairs_h[k][0], pairs_h[k][1]) for k in range(n)]
                todo += [(pairs_h[k][0], pairs_l[k][1]) for k in range(n)]
                todo += [(pairs_l[k][0], pairs_h[k][1]) for k in range(n)]
                for i, (w, m) in enumerate(todo):
                    ins = pe.matmul(outs, w, m, start=first and i == 0, stop=last and i == len(todo) - 1,
                                    skip_group_check=not (first and last))
                return ins

            pe.wait_ge(gate_l_ready, 1)
            pe.wait_ge(xtl_ready, B)
            for half in range(NHALF):
                cols = slice(half * HALF, (half + 1) * HALF)
                three(pb[half][0:NCO + 1, :],
                      [(gate_h[:, k, :], xth[:, k, cols]) for k in range(KC)],
                      [(gate_l[:, k, :], xtl[:, k, cols]) for k in range(KC)], True, True).then_inc(lt_psum, 1)
            pe.wait_ge(lt_ready, 2)
            for b in range(B):
                ins = pe.transpose(pb[2][:, (NCO + 1) * b:(NCO + 1) * (b + 1)], logits_t[:, T * b:T * b + T],
                                   ident[0:NCO + 1, 0:NCO + 1])
            ins.then_inc(logits_psum, 1)
            pe.wait_ge(coef_ready, 1)
            for b in range(B):
                ins = pe.transpose(pb[3][0:PARTS * NCO, :].bitcast(BF16)[:, T * b:T * b + T],
                                   coef_b[:, b, :, :].rearrange("p s e -> p (s e)"), ident_b[:, :])
            ins.then_inc(coef_psum, 1)
            pe.wait_ge(coef_t_ready, 1)

            def up(n, k, cols, tokens, early=False):
                pe.wait_ge(wl_ready, n + 1)
                for part in range(2):
                    if not early:
                        pe.wait_ge([silu_ready, gu_ready][part], n - 1)
                    rows = [slice(256 * c + 128 * part, 256 * c + 128 * part + 128) for c in range(KC)]
                    three([ps_g, ps_u][part][k % 2][:, :],
                          [(w_h[:, k, rows[c]], xth[:, c, cols]) for c in range(KC)],
                          [(w_l[:, k, rows[c]], xtl[:, c, cols]) for c in range(KC)], True, True).then_inc(up_psum, 1)
                if not early:
                    pe.wait_ge(hid_ready, n)
                pe.matmul(ps_c[:, :], sel[:, k, :], coef_t[:, tokens], start=True, stop=True).then_inc(co_psum, 1)

            def down(n, k, last=False):
                pe.wait_ge(hidl_ready, n + 1)
                for m in range(KC):
                    rows = slice(KC * 256 + 128 * m, KC * 256 + 128 * m + 128)
                    ins = three(ps_y[m][:, :], [(w_h[:, k, rows], hid_h[:, k % 2, :])],
                                [(w_l[:, k, rows], hid_l[:, k % 2, :])], False, last)
                ins.then_inc(down_done, 1)

            def open_rows():
                for m in range(KC):
                    pe.matmul(ps_y[m][:, :], zero_b[0:1, 0:128], zero_b[0:1, :], start=True, stop=False,
                              skip_group_check=True)

            def turn_rows(half, pair):
                m = 2 * half + pair
                pe.wait_ge(yt_ready, 2 * half + 2)
                if m:
                    pe.wait_ge(y_ready, m)
                for i in range(2):
                    for k in range(KC):
                        at = T * (2 * pair + i)
                        ins = pe.transpose(ps_t[:, D * i + 128 * k:D * i + 128 * k + 128], y_t[:, k, at:at + T],
                                           ident[:, :])
                ins.then_inc(y_psum, 1)

            def columns(half):
                return slice(half * HALF, (half + 1) * HALF), slice(half * HALF, (half + 1) * HALF)

            up(0, 0, *columns(0), early=True)
            for half in range(NHALF):
                if half:
                    pe.wait_ge(yt_ready, 2 * half)
                open_rows()
                for k in range(RING):
                    if half == 0 or k:
                        pass
                    up(half * NC + k + 1, (k + 1) % RING, *columns(half), early=False)
                    down(half * NC + k, k)
                    if half and k < 2:
                        turn_rows(half - 1, k)
                with pe.Fori(half * NC + RING, (half + 1) * NC - RING, RING) as n:
                    for k in range(RING):
                        up(n + k + 1, (k + 1) % RING, *columns(half))
                        down(n + k, k)
                for k in range(RING):
                    n = (half + 1) * NC - RING + k
                    if k < RING - 1:
                        up(n + 1, k + 1, *columns(half))
                    elif half + 1 < NHALF:
                        up(n + 1, 0, *columns(half + 1))
                    down(n, k, last=k == RING - 1)
            for pair in range(2):
                turn_rows(NHALF - 1, pair)


def bf16_bits(table):
    return (table.astype(np.float32).view(np.uint32) >> 16).astype(np.uint16)


def lay_out(inputs):
    a = {k: np.asarray(v) for k, v in inputs.items()}
    f = np.float32
    got = {"x_in": a["x"], "ctx_in": a["ctx_2048"]}
    got["wqkv_in"] = np.concatenate([a["L0_attn_Wq"], a["L0_attn_Wk"], a["L0_attn_Wv"]], axis=1)
    got["bqkv_in"] = np.concatenate([a["L0_attn_bq"], a["L0_attn_bk"], a["L0_attn_bv"]])
    got["wo_in"] = a["L0_attn_Wo"]
    got["bo_in"] = a["L0_attn_bo"]
    half = DH // 2
    freq = (1.0 / f(10000.0) ** (np.arange(half, dtype=f) * f(2.0) / f(DH))).astype(f)
    angle = (np.arange(T, dtype=f)[:, None] * freq[None, :]).astype(f)
    cos, sin = np.cos(angle).astype(f), np.sin(angle).astype(f)
    heads = ROT // DH
    got["rope_in"] = np.stack([np.tile(np.concatenate([cos, cos], 1), (1, heads)),
                               np.tile(np.concatenate([-sin, sin], 1), (1, heads))], axis=1).astype(f)
    i, j = np.arange(T)[:, None], np.arange(T)[None, :]
    seen = [(i >= j) & ((j >= i - 64) | (j < 4)), i >= j]
    got["masks_in"] = np.stack([np.tile(np.where(s, 0.0, MASKED), (1, BLK)) for s in seen], axis=1)
    got["masks_in"] = bf16_bits(got["masks_in"])
    got["gate_in"] = np.concatenate([a["L0_ffn_gate_w"], a["L0_ffn_sgate_w"], np.zeros((1, D), f)]).T
    none = np.zeros((NC * 128 - HID, D), f)
    w13, shared = a["L0_ffn_w13"], a["L0_ffn_shared_gate_up_w"]
    g = np.concatenate([w13[:, :HE].reshape(-1, D), shared[:HS], none])
    u = np.concatenate([w13[:, HE:].reshape(-1, D), shared[HS:], none])
    d = np.concatenate([a["L0_ffn_w2"].transpose(0, 2, 1).reshape(-1, D), a["L0_ffn_shared_down_w"].T, none])
    gu = np.stack([g.reshape(NC, 128, KC, 128), u.reshape(NC, 128, KC, 128)], axis=1)
    gu = gu.transpose(0, 4, 3, 1, 2).reshape(NC, 128, KC * 256)
    got["chunks_in"] = np.concatenate([gu, d.reshape(NC, 128, D)], axis=2)
    owner = np.minimum(np.arange(NC * 128) // HE, NE)
    one = (owner.reshape(NC, 1, 128) == np.arange(NCO)[None, :, None])
    got["select_in"] = bf16_bits(np.tile(one, (1, PARTS, 1)))
    got["ident_in"] = np.eye(128, dtype=f)
    got["iota_in"] = np.arange(NE, dtype=f)
    return {k: np.ascontiguousarray(v) for k, v in got.items()}


def kernel(**inputs):
    import concourse.bacc as bacc
    from concourse.bass_utils import run_bass_kernel_spmd

    arrays = lay_out(inputs)
    nc = bacc.Bacc("TRN2", target_bir_lowering=False, num_devices=1)
    args = {k: nc.dram_tensor(f"{k}_dram", v.shape, mybir.dt.from_np(v.dtype), kind="ExternalInput").ap()
            for k, v in arrays.items()}
    out = nc.dram_tensor("out_dram", (B, T, D), F32, kind="ExternalOutput").ap()
    decoder_layer(nc, out=out, **args)
    r = run_bass_kernel_spmd(nc, [{f"{k}_dram": v for k, v in arrays.items()}], core_ids=[0])
    return r.results[0]["out_dram"]
```

```python
from contextlib import ExitStack

import numpy as np

import concourse.bass as bass
from concourse import mybir

F32 = mybir.dt.float32
F32R = mybir.dt.float32r
BF16 = mybir.dt.bfloat16
U32 = mybir.dt.uint32
U16 = mybir.dt.uint16
ALU = mybir.AluOpType
ACT = mybir.ActivationFunctionType
AX = mybir.AxisListType

B, T, D = 8, 128, 256
NH, DH, NG = 16, 16, 4
PAD = 32
BLK = 4
TILES = 4
STK = 64
KC = D // 128
QKV = NH * DH + 2 * NG * DH
ROT = NH * DH + NG * DH
TOPK = 4
NE, HE, HS = 16, 176, 704
HID = NE * HE + HS
NC = -(-HID // 128)
RING = 4
PARTS = 3
NCO = NE + 1
HALF = 512
NHALF = B * T // HALF
HB = B // NHALF
WROW = KC * 256 + D
SCALE = DH ** -0.5
EPS = 1e-5
MASKED = -1e30
LATER = (slice(2, 4), slice(4, B))
WARM = (13, 3, 22, 3)


def decoder_layer(nc, x_in, ctx_in, wqkv_in, bqkv_in, wo_in, bo_in, rope_in, masks_in, gate_in,
                  chunks_in, select_in, ident_in, iota_in, out):
    ctx = ExitStack()
    with ctx:
        def sb(name, shape, dt=F32):
            return ctx.enter_context(nc.sbuf_tensor(name, shape, dt))

        def bank(name, dt=F32):
            return ctx.enter_context(nc.psum_tensor(name, [128, 2048 // mybir.dt.size(dt)], dt))

        def sem(name):
            return ctx.enter_context(nc.semaphore(name))

        ident = sb("ident", [128, 128])
        ident_b = sb("ident_b", [128, 128], BF16)
        masks = sb("masks", [128, 2, BLK * 128], BF16)
        rope = sb("rope", [128, 2, ROT])
        wqkv = sb("wqkv", [128, KC, QKV])
        bqkv = sb("bqkv", [128, QKV])
        wo = sb("wo", [128, KC, D])
        bo = sb("bo", [128, D])
        gate = sb("gate", [128, KC, NCO + 1])
        gate_h = sb("gate_h", [128, KC, NCO + 1], F32R)
        gate_l = sb("gate_l", [128, KC, NCO + 1], F32R)
        iota = sb("iota", [128, NE])
        expo = sb("expo", [128, B])
        zero_b = sb("zero_b", [128, HALF], BF16)

        x = sb("x", [128, B + 2, D])
        ctx_sb = sb("ctx_sb", [128, B, D])
        x2 = sb("x2", [128, B, D])
        x3 = sb("x3", [128, B, D])
        stat1 = sb("stat1", [128, B, 6])
        mv1 = sb("mv1", [128, B + 2, 2])
        ve1 = sb("ve1", [128, B])
        rstd1 = sb("rstd1", [128, B + 2])
        xth = sb("xth", [128, KC, B * T], F32R)
        xtl = sb("xtl", [128, KC, B * T], F32R)

        xn1 = sb("xn1", [128, D])
        xt1 = sb("xt1", [128, KC, 128])
        qkv = sb("qkv", [128, QKV])
        turned = sb("turned", [128, ROT])
        swapped = sb("swapped", [128, ROT])
        qk = sb("qk", [128, ROT])
        q_stk = sb("q_stk", [128, NH, STK], F32R)
        k_stk = sb("k_stk", [128, NG, STK], F32R)
        v_pad = sb("v_pad", [128, NG, PAD])
        qt = sb("qt", [128, 2, BLK, 128], F32R)
        kt = sb("kt", [128, 2, 128], F32R)
        xn2 = sb("xn2", [128, D])
        qc_stk = sb("qc_stk", [128, NH, STK], F32R)
        ctx_rows = sb("ctx_rows", [128, D])
        c_stk = sb("c_stk", [128, NH, STK], F32R)
        c_pad = sb("c_pad", [128, BLK, TILES, PAD])
        qtc = sb("qtc", [128, 2, BLK, 128], F32R)
        ktc = sb("ktc", [128, 2, BLK, 128], F32R)
        neg_max = sb("neg_max", [128, TILES, BLK])
        probs = sb("probs", [128, TILES, BLK, 128])
        probs_t = sb("probs_t", [128, TILES, BLK, 128])
        values_t = sb("values_t", [128, BLK, 128])
        inv = sb("inv", [128, NH])
        attn = sb("attn", [128, D])
        attn_t = sb("attn_t", [128, KC, 128])
        values_tc = sb("values_tc", [128, BLK, 128])
        inv_c = sb("inv_c", [128, NH])
        attn_c = sb("attn_c", [128, D])
        stat2 = sb("stat2", [128, 2, 6])
        mv2 = sb("mv2", [128, 2, 2])
        ve2 = sb("ve2", [128, 2])
        rstd2 = sb("rstd2", [128, 2])
        xn3 = sb("xn3", [128, D])
        spare = sb("spare", [128, 4])

        logits_t = sb("logits_t", [NCO + 1, B * T])
        logits = sb("logits", [128, B, NCO])
        top_l = sb("top_l", [128, B])
        ex = sb("ex", [128, B, NE])
        ex_g = sb("ex_g", [128, B])
        ex_g1 = sb("ex_g1", [128, B])
        ex_sum = sb("ex_sum", [128, B])
        ex_inv = sb("ex_inv", [128, B])
        top_v = sb("top_v", [128, B, 8])
        top_i = sb("top_i", [128, B, 8], U32)
        top_f = sb("top_f", [128, B, 8])
        picked = sb("picked", [128, TOPK, B, NE])
        coef = sb("coef", [128, B, NCO])
        coef_r = sb("coef_r", [128, 2, B, NCO])
        coef_b = sb("coef_b", [128, B, PARTS, NCO], BF16)
        coef_t = sb("coef_t", [PARTS * NCO, B * T], BF16)

        w_raw = sb("w_raw", [128, RING, WROW])
        w_h = sb("w_h", [128, RING, WROW], F32R)
        w_l = sb("w_l", [128, RING, WROW], F32R)
        sel = sb("sel", [PARTS * NCO, RING, 128], BF16)
        silu = sb("silu", [128, 2, HALF])
        gu = sb("gu", [128, 2, HALF])
        hid = sb("hid", [128, 2, HALF])
        hid_h = sb("hid_h", [128, 2, HALF], F32R)
        hid_l = sb("hid_l", [128, 2, HALF], F32R)
        y_t = sb("y_t", [128, KC, HALF])

        pb = [bank(f"bank{i}") for i in range(8)]
        ps_s = [pb[g][:, :] for g in range(TILES)]
        ps_x, ps_q, ps_o, ps_w = pb[4], pb[5], pb[6], pb[7]
        ps_g, ps_u, ps_c, ps_y, ps_t = [pb[5], pb[0]], [pb[4], pb[1]], pb[2], [pb[3], pb[6]], pb[7]

        def rows_bank(m):
            return ps_c if m == 3 else ps_t

        x_first = sem("x_first")
        x_rest = sem("x_rest")
        ctx_loaded = sem("ctx_loaded")
        ident_loaded = sem("ident_loaded")
        wqkv_loaded = sem("wqkv_loaded")
        rope_loaded = sem("rope_loaded")
        masks_loaded = sem("masks_loaded")
        wo_loaded = sem("wo_loaded")
        gate_loaded = sem("gate_loaded")
        zeros_ready = sem("zeros_ready")
        pads_ready = sem("pads_ready")
        ident_b_ready = sem("ident_b_ready")
        gate_h_ready = sem("gate_h_ready")
        gate_l_ready = sem("gate_l_ready")
        stats1_ready = sem("stats1_ready")
        var1_ready = sem("var1_ready")
        rstd1_ready = sem("rstd1_ready")
        xb_ready = sem("xb_ready")
        chain1 = sem("chain1")
        xn1_ready = sem("xn1_ready")
        xt1_psum = sem("xt1_psum")
        xt1_ready = sem("xt1_ready")
        qkv_psum = sem("qkv_psum")
        qkv_ready = sem("qkv_ready")
        rope_step = sem("rope_step")
        v_ready = sem("v_ready")
        qk_ready = sem("qk_ready")
        qk_high = sem("qk_high")
        qk_low = sem("qk_low")
        q_psum = sem("q_psum")
        k_psum = sem("k_psum")
        qt_ready = sem("qt_ready")
        kt_ready = sem("kt_ready")
        scores_psum = [sem("scores_psum_s"), sem("scores_psum_c")]
        max_ready = [sem("max_ready_s"), sem("max_ready_c")]
        probs_ready = [sem("probs_ready_s"), sem("probs_ready_c")]
        probs_t_psum = [sem("probs_t_psum_s"), sem("probs_t_psum_c")]
        probs_t_ready = [[sem("probs_t_ready_s0"), sem("probs_t_ready_s1")],
                         [sem("probs_t_ready_c0"), sem("probs_t_ready_c1")]]
        values_psum = [sem("values_psum_s"), sem("values_psum_c")]
        values_taken = [sem("values_taken_s"), sem("values_taken_c")]
        rows_psum = [sem("rows_psum_s"), sem("rows_psum_c")]
        inv_ready = [sem("inv_ready_s"), sem("inv_ready_c")]
        attn_ready = [sem("attn_ready_s"), sem("attn_ready_c")]
        attn_t_psum = sem("attn_t_psum")
        attn_t_ready = sem("attn_t_ready")
        wo_psum = sem("wo_psum")
        x2_ready = sem("x2_ready")
        stat_ready = [sem("stat_ready_s"), sem("stat_ready_c")]
        mv_ready = [sem("mv_ready_s"), sem("mv_ready_c")]
        ve_ready = [sem("ve_ready_s"), sem("ve_ready_c")]
        rstd_ready = [sem("rstd_ready_s"), sem("rstd_ready_c")]
        xn2_ready = sem("xn2_ready")
        xn2_high = sem("xn2_high")
        xn2_low = sem("xn2_low")
        c_pad_ready = sem("c_pad_ready")
        ctx_rows_ready = sem("ctx_rows_ready")
        ctx_high = sem("ctx_high")
        ctx_low = sem("ctx_low")
        ct_psum = sem("ct_psum")
        ktc_ready = sem("ktc_ready")
        qc_psum = sem("qc_psum")
        qtc_ready = sem("qtc_ready")
        x3_ready = sem("x3_ready")
        xn3_ready = sem("xn3_ready")
        xt3_psum = sem("xt3_psum")
        xth_ready = sem("xth_ready")
        xtl_ready = sem("xtl_ready")
        lt_psum = sem("lt_psum")
        lt_ready = sem("lt_ready")
        logits_psum = sem("logits_psum")
        route = sem("route")
        shifted_ready = sem("shifted_ready")
        exps_ready = sem("exps_ready")
        coef_ready = sem("coef_ready")
        coef_psum = sem("coef_psum")
        coef_t_ready = sem("coef_t_ready")
        w_loaded = [sem(f"w_loaded{r}") for r in range(RING)]
        wh_ready = sem("wh_ready")
        wl_ready = sem("wl_ready")
        up_psum = sem("up_psum")
        co_psum = sem("co_psum")
        silu_ready = sem("silu_ready")
        gu_ready = sem("gu_ready")
        hid_ready = sem("hid_ready")
        hidh_ready = sem("hidh_ready")
        hidl_ready = sem("hidl_ready")
        down_done = sem("down_done")
        yt_ready = sem("yt_ready")
        y_psum = sem("y_psum")
        y_ready = sem("y_ready")
        y_stored = sem("y_stored")

        block = ctx.enter_context(nc.Block())
        SELF, CROSS = 0, 1

        def store(sp, half, pair):
            m = 2 * half + pair
            sp.wait_ge(y_ready, m + 1)
            b = m * 2
            sp.dma_start(out[b:b + 2].rearrange("b p d -> p b d"), x3[:, b:b + 2, :]).then_inc(y_stored, 16)

        @block.sync
        def _(sp):
            sp.dma_start(x[:, 0:2, :], x_in[0:2].rearrange("b p d -> p b d")).then_inc(x_first, 16)
            sp.dma_start(wqkv[:, :, :], wqkv_in.rearrange("(k p) n -> p k n", p=128)).then_inc(wqkv_loaded, 16)
            sp.dma_start(rope[:, :, :], rope_in).then_inc(rope_loaded, 16)
            sp.dma_start(x[:, 2:B, :], x_in[2:B].rearrange("b p d -> p b d")).then_inc(x_rest, 16)
            sp.dma_start(ctx_sb[:, :, :], ctx_in.rearrange("b p d -> p b d")).then_inc(ctx_loaded, 16)
            sp.dma_start(gate[:, :, :], gate_in.rearrange("(k p) n -> p k n", p=128)).then_inc(gate_loaded, 16)
            sp.dma_start(iota[:, :], iota_in.partition_broadcast(128)).then_inc(gate_loaded, 16)

            def load_chunk(n, c, r):
                if not isinstance(n, int) or n >= RING:
                    sp.wait_ge(wl_ready, n - RING + 1)
                    sp.wait_ge(co_psum, n - RING + 1)
                sp.dma_start(w_raw[:, r, :], chunks_in[bass.ds(c, 1)].rearrange("c p n -> p (c n)")).then_inc(w_loaded[r], 16)
                sp.dma_start(sel[:, r, :].bitcast(U16), select_in[bass.ds(c, 1)].rearrange("c p n -> p (c n)")).then_inc(w_loaded[r], 16)

            for half in range(NHALF):
                for r in range(RING):
                    load_chunk(half * NC + r, r, r)
                with sp.Fori(1, NC // RING) as turn:
                    for r in range(RING):
                        load_chunk(turn * RING + (half * NC + r), turn * RING + r, r)
            for half in range(NHALF):
                for pair in range(2):
                    store(sp, half, pair)
            sp.wait_ge(y_stored, 16 * NHALF * 2)

        @block.gpsimd
        def _(pool):
            pool.memset(zero_b[:, :], 0.0).then_inc(zeros_ready, 1)
            pool.memset(expo[:, :], -0.5).then_inc(pads_ready, 1)
            pool.memset(q_stk[:, :, :].bitcast(F32), 0.0).then_inc(pads_ready, 1)
            pool.memset(k_stk[:, :, :].bitcast(F32), 0.0).then_inc(pads_ready, 1)
            pool.memset(v_pad[:, :, :], 1.0).then_inc(pads_ready, 1)
            pool.wait_ge(pads_ready, 4)
            pool.wait_ge(var1_ready, 1)
            pool.tensor_tensor(rstd1[:, 0:2], ve1[:, 0:2], expo[:, 0:2], ALU.pow).then_inc(rstd1_ready, 1)
            pool.wait_ge(ident_loaded, 16)
            pool.tensor_copy(ident_b[:, :], ident[:, :]).then_inc(ident_b_ready, 1)

            def turn(f):
                pool.wait_ge(qkv_ready, f + 1)
                halves = qkv[:, 0:ROT].rearrange("p (h s i) -> p h s i", s=2, i=DH // 2)
                sines = rope[:, 1, :].rearrange("p (h s i) -> p h s i", s=2, i=DH // 2)
                other = swapped[:, :].rearrange("p (h s i) -> p h s i", s=2, i=DH // 2)
                pool.tensor_tensor(turned[:, :], qkv[:, 0:ROT], rope[:, 0, :], ALU.mult).then_inc(rope_step, 1)
                pool.tensor_tensor(other[:, :, 0, :], halves[:, :, 1, :], sines[:, :, 0, :], ALU.mult).then_inc(rope_step, 1)
                pool.tensor_tensor(other[:, :, 1, :], halves[:, :, 0, :], sines[:, :, 1, :], ALU.mult).then_inc(rope_step, 1)
                pool.wait_ge(rope_step, 3 * (f + 1))
                if not isinstance(f, int) or f:
                    pool.wait_ge(qk_low, 2 * f)
                pool.tensor_tensor(qk[:, :], turned[:, :], swapped[:, :], ALU.add).then_inc(qk_ready, 1)

            pool.wait_ge(rope_loaded, 32)
            turn(0)
            pool.memset(rstd1[:, B:B + 2], 0.0).then_inc(pads_ready, 1)
            pool.memset(mv1[:, B:B + 2, :], 0.0).then_inc(pads_ready, 1)
            pool.memset(qc_stk[:, :, :].bitcast(F32), 0.0).then_inc(pads_ready, 1)
            pool.memset(c_stk[:, :, :].bitcast(F32), 0.0).then_inc(pads_ready, 1)
            pool.memset(c_pad[:, :, :, :], 1.0).then_inc(pads_ready, 1)
            pool.memset(x[:, B:B + 2, :], 0.0).then_inc(pads_ready, 1)
            pool.wait_ge(x_first, 16)
            pool.wait_ge(x_rest, 16)
            pool.wait_ge(wo_loaded, 32)
            for b in range(B):
                ins = pool.tensor_tensor(x2[:, b, :], x[:, b, :], bo[:, :], ALU.add)
            ins.then_inc(xb_ready, 1)
            pool.wait_ge(ctx_loaded, 16)
            pool.wait_ge(pads_ready, 10)

            def inverse_deviation(kind, b):
                pool.wait_ge(ve_ready[kind], b + 1)
                pool.tensor_tensor(rstd2[:, kind:kind + 1], ve2[:, kind:kind + 1], expo[:, 0:1], ALU.pow
                                   ).then_inc(rstd_ready[kind], 1)

            def pad_context(c):
                if not isinstance(c, int) or c:
                    pool.wait_ge(values_psum[CROSS], 2 * c)
                pool.tensor_copy(c_pad[:, :, :, 0:DH],
                                 ctx_sb[:, bass.ds(c, 1), :].rearrange("p b (j g d) -> p (b j) g d", j=BLK, g=TILES)
                                 ).then_inc(c_pad_ready, 1)

            def stack_context(c):
                first = isinstance(c, int) and c == 0
                source = ctx_sb[:, bass.ds(c, 1), :]
                parts = c_stk[:, :, :].rearrange("p h (s d) -> p h s d", d=DH)
                if not first:
                    pool.wait_ge(ct_psum, 2 * c)
                    pool.wait_ge(ctx_low, c)
                pool.tensor_copy(parts[:, :, 0:3:2, :], source.rearrange("p b (h d) -> p (b h) d", h=NH)
                                 .unsqueeze(2).broadcast_to([128, NH, 2, DH])).then_inc(ctx_high, 1)
                pool.tensor_copy(ctx_rows[:, :], source.rearrange("p b d -> p (b d)")).then_inc(ctx_rows_ready, 1)
                pool.wait_ge(ctx_high, c + 1)
                pool.wait_ge(ctx_rows_ready, c + 1)
                pool.tensor_tensor(parts[:, :, 1, :], ctx_rows[:, :].rearrange("p (h d) -> p h d", h=NH),
                                   parts[:, :, 0, :].bitcast(F32), ALU.subtract).then_inc(ctx_low, 1)

            def iteration(t, cross_on, tail_on):
                if cross_on:
                    pad_context(t - 1)
                turn(t + 1)
                if tail_on:
                    inverse_deviation(CROSS, t - 2)
                stack_context(t)
                if not tail_on:
                    pool.wait_ge(var1_ready, 2 + t)
                    pool.tensor_tensor(rstd1[:, LATER[t]], ve1[:, LATER[t]], expo[:, LATER[t]], ALU.pow
                                       ).then_inc(rstd1_ready, 1)
                inverse_deviation(SELF, t)

            iteration(0, False, False)
            iteration(1, True, False)
            with pool.Fori(2, B) as t:
                iteration(t, True, True)
            pad_context(B - 1)
            inverse_deviation(CROSS, B - 2)

            def low_part(n, r):
                pool.wait_ge(wh_ready, n + 1)
                pool.tensor_tensor(w_l[:, r, :], w_raw[:, r, :], w_h[:, r, :].bitcast(F32), ALU.subtract
                                   ).then_inc(wl_ready, 1)

            low_part(0, 0)
            low_part(1, 1)
            low_part(2, 2)
            low_part(3, 3)
            inverse_deviation(CROSS, B - 1)
            with pool.Fori(RING, NHALF * NC, RING) as n:
                for r in range(RING):
                    low_part(n + r, r)

        @block.scalar
        def _(act):
            act.dma_start(ident[:, :], ident_in).then_inc(ident_loaded, 16)
            act.dma_start(bqkv[:, :], bqkv_in.partition_broadcast(128)).then_inc(rope_loaded, 16)
            act.dma_start(masks[:, :, :].bitcast(U16), masks_in).then_inc(masks_loaded, 16)
            act.dma_start(bo[:, :], bo_in.partition_broadcast(128)).then_inc(wo_loaded, 16)
            act.dma_start(wo[:, :, :], wo_in.rearrange("(k p) n -> p k n", p=128)).then_inc(wo_loaded, 16)

            def front_a(f):
                act.wait_ge(xt1_psum, f + 1)
                act.activation(xt1[:, :, :], ps_w[:, 0:KC * 128].rearrange("p (k n) -> p k n", k=KC), ACT.Copy
                               ).then_inc(xt1_ready, 1)

            def front_c(f, u):
                act.wait_ge(q_psum, 2 * f + u + 1)
                act.activation(qt[:, u, :, :], ps_q[:, :].rearrange("p (j n) -> p j n", j=BLK), ACT.Copy, scale=SCALE
                               ).then_inc(qt_ready, 1)

            def cross_q(c, u):
                act.wait_ge(qc_psum, 2 * c + u + 1)
                act.activation(qtc[:, u, :, :], ps_q[:, :].rearrange("p (j n) -> p j n", j=BLK), ACT.Copy, scale=SCALE
                               ).then_inc(qtc_ready, 1)

            def cross_k(c, u):
                act.wait_ge(ct_psum, 2 * c + u + 1)
                act.activation(ktc[:, u, :, :], ps_x[:, :].rearrange("p (j n) -> p j n", j=BLK), ACT.Copy
                               ).then_inc(ktc_ready, 1)

            def exps(kind, b, u):
                for g in (2 * u, 2 * u + 1):
                    act.wait_ge(max_ready[kind], 4 * b + g + 1)
                    for j in range(BLK):
                        ins = act.activation(probs[:, g, j, :], ps_s[g][:, 128 * j:128 * j + 128], ACT.Exp,
                                             bias=neg_max[:, g, j:j + 1])
                    ins.then_inc(probs_ready[kind], 1)

            def take_probs_t(kind, b, g):
                act.wait_ge(probs_t_psum[kind], 4 * b + g + 1)
                act.activation(probs_t[:, g, :, :], ps_s[g].rearrange("p (j n) -> p j n", j=BLK), ACT.Copy
                               ).then_inc(probs_t_ready[kind][g // 2], 1)

            def take_values(kind, b):
                act.wait_ge(values_psum[kind], 2 * b + 2)
                act.activation((values_t if kind == SELF else values_tc)[:, :, :],
                               ps_o[:, :].rearrange("p (j n) -> p j n", j=BLK), ACT.Copy).then_inc(values_taken[kind], 1)

            def take_attn_t(b):
                act.wait_ge(attn_t_psum, b + 1)
                act.activation(attn_t[:, :, :], ps_x[:, 0:KC * 128].rearrange("p (k n) -> p k n", k=KC), ACT.Copy
                               ).then_inc(attn_t_ready, 1)

            def take_xth(b, source):
                act.wait_ge(xt3_psum, b + 1)
                act.activation(xth[:, :, bass.ds(b * T, T)],
                               source[:, 0:KC * 128].rearrange("p (k n) -> p k n", k=KC), ACT.Copy
                               ).then_inc(xth_ready, 1)

            def take_logits_t(half):
                act.wait_ge(lt_psum, half + 1)
                act.activation(logits_t[:, half * HALF:(half + 1) * HALF], ps_w[0:NCO + 1, :], ACT.Copy
                               ).then_inc(lt_ready, 1)

            def route_exps(half):
                bs = slice(half * HB, (half + 1) * HB)
                act.wait_ge(shifted_ready, half + 1)
                act.activation(ex[:, bs, :], ex[:, bs, :], ACT.Exp).then_inc(exps_ready, 1)
                act.activation(ex_g[:, bs], logits[:, bs, NE], ACT.Exp, scale=-1.0).then_inc(exps_ready, 1)

            def take_coefs(half):
                act.wait_ge(coef_psum, half + 1)
                act.activation(coef_t[:, half * HALF:(half + 1) * HALF], ps_w[0:PARTS * NCO, :].bitcast(BF16)[:, 0:HALF],
                               ACT.Copy).then_inc(coef_t_ready, 1)

            def iteration(t, cross_on, tail_on):
                if tail_on:
                    take_values(CROSS, t - 2)
                exps(SELF, t, 0)
                front_a(t + 1)
                if cross_on:
                    cross_k(t - 1, 0)
                    cross_q(t - 1, 0)
                exps(SELF, t, 1)
                if cross_on:
                    cross_k(t - 1, 1)
                    cross_q(t - 1, 1)
                take_probs_t(SELF, t, 2)
                take_values(SELF, t)
                if cross_on:
                    exps(CROSS, t - 1, 0)
                if tail_on:
                    take_xth(t - 2, ps_x)
                if cross_on:
                    exps(CROSS, t - 1, 1)
                take_attn_t(t)
                front_c(t + 1, 0)
                if cross_on:
                    take_probs_t(CROSS, t - 1, 2)
                front_c(t + 1, 1)

            front_a(0)
            front_c(0, 0)
            front_c(0, 1)
            iteration(0, False, False)
            iteration(1, True, False)
            with act.Fori(2, B) as t:
                iteration(t, True, True)

            def high_part(n, r, m):
                act.wait_ge(w_loaded[r], 32 * (m + 1))
                if not isinstance(n, int) or n >= RING:
                    act.wait_ge(down_done, n - RING + 1)
                act.activation(w_h[:, r, :], w_raw[:, r, :], ACT.Copy).then_inc(wh_ready, 1)

            high_part(0, 0, 0)
            take_values(CROSS, B - 2)
            take_logits_t(0)
            for u in range(2):
                cross_k(B - 1, u)
                cross_q(B - 1, u)
            high_part(1, 1, 0)
            high_part(2, 2, 0)
            take_xth(B - 2, ps_x)
            exps(CROSS, B - 1, 0)
            route_exps(0)
            exps(CROSS, B - 1, 1)
            take_probs_t(CROSS, B - 1, 1)
            take_probs_t(CROSS, B - 1, 2)

            def gate(n, k):
                act.wait_ge(up_psum, 2 * n + 1)
                if not isinstance(n, int) or n >= 2:
                    act.wait_ge(gu_ready, n - 1)
                act.activation(silu[:, k % 2, :], ps_g[k % 2][:, :], ACT.Silu).then_inc(silu_ready, 1)

            def high_hidden(n, k):
                act.wait_ge(hid_ready, n + 1)
                if not isinstance(n, int) or n >= 2:
                    act.wait_ge(down_done, n - 1)
                act.activation(hid_h[:, k % 2, :], hid[:, k % 2, :], ACT.Copy).then_inc(hidh_ready, 1)

            def chunk(n, k, q, ahead=True, gate_first=False):
                if gate_first:
                    gate(n, k)
                if ahead:
                    r = (k + 2) % RING
                    high_part(n + 2, r, q + (k + 2) // RING)
                if not gate_first:
                    gate(n, k)
                high_hidden(n, k)

            gate(0, 0)
            take_coefs(0)
            take_values(CROSS, B - 1)

            def take_y(half):
                act.wait_ge(down_done, (half + 1) * NC)
                act.activation(y_t[:, 0, :], ps_y[0][:, :], ACT.Copy).then_inc(yt_ready, 1)

            turns = NC // RING
            high_hidden(0, 0)
            for k in range(1, RING):
                chunk(k, k, 0)
                if k == 1:
                    take_xth(B - 1, ps_w)
                if k == 2:
                    take_logits_t(1)
            for k in range(RING):
                chunk(RING + k, k, 1, gate_first=k == 1)
                if k == 0:
                    route_exps(1)
            with act.Fori(2, turns - 1) as q:
                for k in range(RING):
                    chunk(q * RING + k, k, q)
            for k in range(RING):
                chunk(NC - RING + k, k, turns - 1)
                if k == 2:
                    take_coefs(1)
            for k in range(RING):
                chunk(NC + k, k, turns)
                if k == 0:
                    take_y(0)
            with act.Fori(turns + 1, 2 * turns - 1) as q:
                for k in range(RING):
                    chunk(q * RING + k, k, q)
            for k in range(RING):
                chunk(2 * NC - RING + k, k, 2 * turns - 1, ahead=k < RING - 2)
            take_y(1)

        @block.vector
        def _(dve):
            def one(ap, i):
                return ap[:, bass.ds(i, 1), :].rearrange("p b d -> p (b d)")

            links = [0]

            def link(ins):
                links[0] += 1
                ins.then_inc(chain1, 1)
                dve.wait_ge(chain1, links[0])

            def first_norms(bs):
                done = bs.start
                for b in range(bs.start, bs.stop):
                    dve.bn_stats(stat1[:, b, :], x[:, b, :]).then_inc(stats1_ready, 1)
                for b in range(bs.start, bs.stop):
                    dve.wait_ge(stats1_ready, done + b + 1)
                    dve.bn_aggr(mv1[:, b, :], stat1[:, b, :]).then_inc(stats1_ready, 1)
                dve.wait_ge(stats1_ready, 2 * bs.stop)
                dve.tensor_scalar(ve1[:, bs], mv1[:, bs, 1], EPS, None, ALU.add).then_inc(var1_ready, 1)

            def front_n(f):
                if not isinstance(f, int) or f:
                    dve.wait_ge(xt1_psum, f)
                dve.tensor_scalar(xn1[:, :], one(x, f), mv1[:, bass.ds(f, 1), 0], rstd1[:, bass.ds(f, 1)], ALU.subtract, ALU.mult).then_inc(xn1_ready, 1)

            def front_r(f):
                dve.wait_ge(qkv_psum, f + 1)
                dve.tensor_tensor(qkv[:, :], ps_w[:, 0:QKV], bqkv[:, :], ALU.add).then_inc(qkv_ready, 1)

            def stacks():
                nq = NH * DH
                return (qk[:, 0:nq].rearrange("p (h d) -> p h d", h=NH), qk[:, nq:ROT].rearrange("p (h d) -> p h d", h=NG),
                        q_stk[:, :, :].rearrange("p h (s d) -> p h s d", d=DH),
                        k_stk[:, :, :].rearrange("p h (s d) -> p h s d", d=DH))

            def front_p(f):
                queries, keys, q_parts, k_parts = stacks()
                dve.wait_ge(qk_ready, f + 1)
                dve.tensor_copy(q_parts[:, :, 0:2, :], queries.unsqueeze(2).broadcast_to([128, NH, 2, DH])
                                ).then_inc(qk_high, 1)
                dve.tensor_copy(k_parts[:, :, 0:3:2, :], keys.unsqueeze(2).broadcast_to([128, NG, 2, DH])
                                ).then_inc(qk_high, 1)

            def front_l(f):
                queries, keys, q_parts, k_parts = stacks()
                dve.wait_ge(qk_high, 2 * f + 2)
                dve.tensor_tensor(q_parts[:, :, 2, :], queries, q_parts[:, :, 0, :].bitcast(F32), ALU.subtract
                                  ).then_inc(qk_low, 1)
                dve.tensor_tensor(k_parts[:, :, 1, :], keys, k_parts[:, :, 0, :].bitcast(F32), ALU.subtract
                                  ).then_inc(qk_low, 1)

            def front_v(f):
                if not isinstance(f, int) or f:
                    dve.wait_ge(values_psum[SELF], 2 * f)
                dve.tensor_copy(v_pad[:, :, 0:DH], qkv[:, ROT:QKV].rearrange("p (g d) -> p g d", g=NG)
                                ).then_inc(v_ready, 1)

            def front_k(f):
                dve.wait_ge(k_psum, f + 1)
                dve.tensor_copy(kt[:, :, :], ps_w[:, 0:256].rearrange("p (u n) -> p u n", u=2)).then_inc(kt_ready, 1)

            def row_max(kind, b, u):
                for g in (2 * u, 2 * u + 1):
                    dve.wait_ge(scores_psum[kind], 4 * b + g + 1)
                    dve.tensor_reduce(neg_max[:, g, :], ps_s[g].rearrange("p (j n) -> p j n", j=BLK), AX.X, ALU.max,
                                      negate=True).then_inc(max_ready[kind], 1)

            def take_probs_t(kind, b, g):
                dve.wait_ge(probs_t_psum[kind], 4 * b + g + 1)
                dve.tensor_copy(probs_t[:, g, :, :], ps_s[g].rearrange("p (j n) -> p j n", j=BLK)
                                ).then_inc(probs_t_ready[kind][g // 2], 1)

            def normalise(kind, b, inverse, result):
                dve.wait_ge(rows_psum[kind], b + 1)
                heads = ps_o[:, :].rearrange("p (h c) -> p h c", h=NH)
                dve.reciprocal(inverse[:, :], heads[:, :, DH]).then_inc(inv_ready[kind], 1)
                dve.wait_ge(inv_ready[kind], b + 1)
                if kind == SELF:
                    heads = heads.rearrange("p (j g) c -> p j g c", j=BLK)
                    dve.tensor_tensor(result[:, :].rearrange("p (g j d) -> p j g d", g=NG, j=BLK), heads[:, :, :, 0:DH],
                                      inverse[:, :].rearrange("p (j g) -> p j g", j=BLK).unsqueeze(3).broadcast_to([128, BLK, NG, DH]),
                                      ALU.mult).then_inc(attn_ready[kind], 1)
                else:
                    dve.tensor_tensor(result[:, :].rearrange("p (h d) -> p h d", h=NH), heads[:, :, 0:DH],
                                      inverse[:, :].unsqueeze(2).broadcast_to([128, NH, DH]), ALU.mult
                                      ).then_inc(attn_ready[kind], 1)

            def carry_wait(i):
                dve.memset(spare[:, i:i + 1], 0.0)

            def statistics(kind, b):
                rows, rows_ready = ((x2, x2_ready), (x3, x3_ready))[kind]
                dve.wait_ge(rows_ready, b + 1)
                carry_wait(2 * kind)
                dve.bn_stats(stat2[:, kind, :], one(rows, b)).then_inc(stat_ready[kind], 1)
                dve.wait_ge(stat_ready[kind], b + 1)
                carry_wait(2 * kind + 1)
                dve.bn_aggr(mv2[:, kind, :], stat2[:, kind, :]).then_inc(mv_ready[kind], 1)
                dve.wait_ge(mv_ready[kind], b + 1)
                dve.tensor_scalar(ve2[:, kind:kind + 1], mv2[:, kind, 1:2], EPS, None, ALU.add
                                  ).then_inc(ve_ready[kind], 1)

            def cross_rows(b):
                normalise(CROSS, b, inv_c, attn_c)
                dve.wait_ge(attn_ready[CROSS], b + 1)
                dve.tensor_tensor(one(x3, b), attn_c[:, :], one(x2, b), ALU.add).then_inc(x3_ready, 1)

            def third_norm(b):
                dve.wait_ge(rstd_ready[CROSS], b + 1)
                dve.tensor_scalar(xn3[:, :], one(x3, b), mv2[:, CROSS, 0:1], rstd2[:, CROSS:CROSS + 1],
                                  ALU.subtract, ALU.mult).then_inc(xn3_ready, 1)

            def second_norm(b):
                dve.wait_ge(rstd_ready[SELF], b + 1)
                dve.tensor_scalar(xn2[:, :], one(x2, b), mv2[:, SELF, 0:1], rstd2[:, SELF:SELF + 1],
                                  ALU.subtract, ALU.mult).then_inc(xn2_ready, 1)

            def stack_queries(b):
                queries = xn2[:, :].rearrange("p (h d) -> p h d", h=NH)
                parts = qc_stk[:, :, :].rearrange("p h (s d) -> p h s d", d=DH)
                dve.wait_ge(xn2_ready, b + 1)
                dve.tensor_copy(parts[:, :, 0:2, :], queries.unsqueeze(2).broadcast_to([128, NH, 2, DH])
                                ).then_inc(xn2_high, 1)
                dve.wait_ge(xn2_high, b + 1)
                dve.tensor_tensor(parts[:, :, 2, :], queries, parts[:, :, 0, :].bitcast(F32), ALU.subtract
                                  ).then_inc(xn2_low, 1)

            def take_xtl(b, source):
                dve.wait_ge(xth_ready, b + 1)
                cols = bass.ds(b * T, T)
                dve.tensor_tensor(xtl[:, :, cols], source[:, 0:KC * 128].rearrange("p (k n) -> p k n", k=KC),
                                  xth[:, :, cols].bitcast(F32), ALU.subtract).then_inc(xtl_ready, 1)

            def iteration(t, cross_on, tail_on):
                if cross_on:
                    second_norm(t - 1)
                row_max(SELF, t, 0)
                if cross_on:
                    stack_queries(t - 1)
                row_max(SELF, t, 1)
                if tail_on:
                    cross_rows(t - 2)
                take_probs_t(SELF, t, 0)
                front_r(t + 1)
                take_probs_t(SELF, t, 1)
                if tail_on:
                    statistics(CROSS, t - 2)
                take_probs_t(SELF, t, 3)
                if cross_on:
                    row_max(CROSS, t - 1, 0)
                if tail_on:
                    third_norm(t - 2)
                front_p(t + 1)
                front_l(t + 1)
                if cross_on:
                    row_max(CROSS, t - 1, 1)
                if tail_on:
                    take_xtl(t - 2, ps_x)
                normalise(SELF, t, inv, attn)
                if cross_on:
                    take_probs_t(CROSS, t - 1, 0)
                front_k(t + 1)
                if cross_on:
                    take_probs_t(CROSS, t - 1, 1)
                front_v(t + 1)
                if cross_on:
                    take_probs_t(CROSS, t - 1, 3)
                if not tail_on:
                    dve.wait_ge(x_rest, 16)
                    first_norms(LATER[t])
                dve.wait_ge(wo_psum, t + 1)
                if isinstance(t, int):
                    dve.wait_ge(xb_ready, 1)
                dve.tensor_tensor(one(x2, t), ps_w[:, 0:D], one(x2, t), ALU.add).then_inc(x2_ready, 1)
                statistics(SELF, t)
                if isinstance(t, int):
                    dve.wait_ge(rstd1_ready, 2)
                front_n(t + 2)

            dve.wait_ge(x_first, 16)
            first_norms(slice(0, 2))
            dve.wait_ge(rstd1_ready, 1)
            front_n(0)
            dve.wait_ge(rope_loaded, 32)
            front_r(0)
            dve.wait_ge(pads_ready, 4)
            front_p(0)
            front_l(0)
            front_v(0)
            front_k(0)
            front_n(1)
            iteration(0, False, False)
            dve.wait_ge(pads_ready, 10)
            dve.wait_ge(gate_loaded, 32)
            dve.tensor_copy(gate_h[:, :, :], gate[:, :, :]).then_inc(gate_h_ready, 1)
            dve.wait_ge(gate_h_ready, 1)
            dve.tensor_tensor(gate_l[:, :, :], gate[:, :, :], gate_h[:, :, :].bitcast(F32), ALU.subtract
                              ).then_inc(gate_l_ready, 1)
            iteration(1, True, False)
            dve.wait_ge(rstd1_ready, 3)
            with dve.Fori(2, B) as t:
                iteration(t, True, True)

            def over(ap, n):
                return ap.unsqueeze(2).broadcast_to([128, HB, n])

            def route_shift(half):
                bs = slice(half * HB, (half + 1) * HB)
                dve.wait_ge(logits_psum, half + 1)
                link(dve.tensor_copy(logits[:, bs, :],
                                     ps_w[:, 0:HB * (NCO + 1)].rearrange("p (b e) -> p b e", b=HB)[:, :, 0:NCO]))
                link(dve.tensor_reduce(top_l[:, bs], logits[:, bs, 0:NE], AX.X, ALU.max))
                dve.tensor_tensor(ex[:, bs, :], logits[:, bs, 0:NE], over(top_l[:, bs], NE), ALU.subtract
                                  ).then_inc(shifted_ready, 1)

            def route_top(half):
                bs = slice(half * HB, (half + 1) * HB)
                dve.wait_ge(exps_ready, 2 * half + 2)
                dve.tensor_scalar(ex_g1[:, bs], ex_g[:, bs], 1.0, None, ALU.add).then_inc(chain1, 1)
                dve.tensor_reduce(ex_sum[:, bs], ex[:, bs, :], AX.X, ALU.add).then_inc(chain1, 1)
                links[0] += 2
                for b in range(bs.start, bs.stop):
                    dve.max(top_v[:, b, :], ex[:, b, :]).then_inc(route, 1)
                for b in range(bs.start, bs.stop):
                    dve.wait_ge(route, 2 * bs.start + b - bs.start + 1)
                    dve.max_index(top_i[:, b, :], top_v[:, b, :], ex[:, b, :]).then_inc(route, 1)
                dve.wait_ge(chain1, links[0])
                dve.reciprocal(ex_inv[:, bs], ex_sum[:, bs]).then_inc(chain1, 1)
                dve.reciprocal(coef[:, bs, NE], ex_g1[:, bs]).then_inc(chain1, 1)
                links[0] += 2
                dve.wait_ge(route, 2 * bs.stop)
                link(dve.tensor_copy(top_f[:, bs, :], top_i[:, bs, :]))

            def route_pick(half):
                bs = slice(half * HB, (half + 1) * HB)
                for k in range(TOPK):
                    dve.tensor_tensor(picked[:, k, bs, :], iota[:, :].unsqueeze(1).broadcast_to([128, HB, NE]),
                                      over(top_f[:, bs, k], NE), ALU.is_equal).then_inc(chain1, 1)
                    links[0] += 1
                dve.wait_ge(chain1, links[0])
                for k in range(TOPK):
                    dve.tensor_tensor(picked[:, k, bs, :], picked[:, k, bs, :], over(top_v[:, bs, k], NE), ALU.mult
                                      ).then_inc(chain1, 1)
                    links[0] += 1
                dve.wait_ge(chain1, links[0])

            def route_sum(half):
                bs = slice(half * HB, (half + 1) * HB)
                link(dve.tensor_tensor(picked[:, 0:2, bs, :], picked[:, 0:2, bs, :], picked[:, 2:4, bs, :], ALU.add))
                link(dve.tensor_tensor(picked[:, 0, bs, :], picked[:, 0, bs, :], picked[:, 1, bs, :], ALU.add))
                link(dve.tensor_tensor(coef[:, bs, 0:NE], picked[:, 0, bs, :], over(ex_inv[:, bs], NE), ALU.mult))

            def route_parts(half):
                bs = slice(half * HB, (half + 1) * HB)
                link(dve.tensor_copy(coef_b[:, bs, 0, :], coef[:, bs, :]))
                link(dve.tensor_tensor(coef_r[:, 0, bs, :], coef[:, bs, :], coef_b[:, bs, 0, :], ALU.subtract))
                link(dve.tensor_copy(coef_b[:, bs, 1, :], coef_r[:, 0, bs, :]))
                link(dve.tensor_tensor(coef_r[:, 1, bs, :], coef_r[:, 0, bs, :], coef_b[:, bs, 1, :], ALU.subtract))
                dve.tensor_copy(coef_b[:, bs, 2, :], coef_r[:, 1, bs, :]).then_inc(coef_ready, 1)

            def gated(n, k):
                dve.wait_ge(silu_ready, n + 1)
                dve.wait_ge(up_psum, 2 * n + 2)
                dve.tensor_tensor(gu[:, k % 2, :], silu[:, k % 2, :], ps_u[k % 2][:, :], ALU.mult).then_inc(gu_ready, 1)

            second_norm(B - 1)
            stack_queries(B - 1)
            cross_rows(B - 2)
            statistics(CROSS, B - 2)
            third_norm(B - 2)
            route_shift(0)
            row_max(CROSS, B - 1, 0)
            take_xtl(B - 2, ps_x)
            row_max(CROSS, B - 1, 1)
            route_top(0)
            take_probs_t(CROSS, B - 1, 0)
            take_probs_t(CROSS, B - 1, 3)
            route_pick(0)
            route_sum(0)
            route_parts(0)
            gated(0, 0)

            def chunk(n, k):
                if not isinstance(n, int) or n >= 2:
                    gated(n, k)
                dve.wait_ge(gu_ready, n + 1)
                dve.wait_ge(co_psum, n + 1)
                if not isinstance(n, int) or n >= 2:
                    dve.wait_ge(hidl_ready, n - 1)
                dve.tensor_tensor(hid[:, k % 2, :], gu[:, k % 2, :], ps_c[:, :], ALU.mult).then_inc(hid_ready, 1)
                dve.wait_ge(hidh_ready, n + 1)
                dve.tensor_tensor(hid_l[:, k % 2, :], hid[:, k % 2, :], hid_h[:, k % 2, :].bitcast(F32), ALU.subtract
                                  ).then_inc(hidl_ready, 1)

            def finish(half):
                dve.wait_ge(down_done, (half + 1) * NC)
                dve.tensor_copy(y_t[:, 1, :], ps_y[1][:, :]).then_inc(yt_ready, 1)

            def sum_rows(half, pair):
                m = 2 * half + pair
                dve.wait_ge(y_psum, m + 1)
                dve.tensor_tensor(x3[:, 2 * m:2 * m + 2, :], rows_bank(m)[:, :].rearrange("p (b d) -> p b d", b=2),
                                  x3[:, 2 * m:2 * m + 2, :], ALU.add).then_inc(y_ready, 1)

            for k in range(RING):
                chunk(k, k)
                if k == 0:
                    cross_rows(B - 1)
                    statistics(CROSS, B - 1)
                    gated(1, 1)
                    third_norm(B - 1)
                if k == 1:
                    take_xtl(B - 1, ps_w)
                if k == 3:
                    route_shift(1)
            for k in range(RING):
                chunk(RING + k, k)
                if k == 1:
                    route_top(1)
                if k == 2:
                    route_pick(1)
                    route_sum(1)
                if k == 3:
                    route_parts(1)
            with dve.Fori(2 * RING, NC, RING) as n:
                for k in range(RING):
                    chunk(n + k, k)
            for k in range(RING):
                chunk(NC + k, k)
                if k == 0:
                    finish(0)
                if 1 <= k < 3:
                    sum_rows(0, k - 1)
            with dve.Fori(NC + RING, 2 * NC, RING) as n:
                for k in range(RING):
                    chunk(n + k, k)
            finish(1)
            for pair in range(2):
                sum_rows(1, pair)

        @block.tensor
        def _(pe):
            def front_a(f):
                pe.wait_ge(xn1_ready, f + 1)
                if not isinstance(f, int) or f >= 2:
                    pe.wait_ge(x2_ready, f - 1)
                for k in range(KC):
                    ins = pe.transpose(ps_w[:, 128 * k:128 * k + 128], xn1[:, 128 * k:128 * k + 128], ident[:, :])
                ins.then_inc(xt1_psum, 1)

            def front_b(f):
                pe.wait_ge(xt1_ready, f + 1)
                for k in range(KC):
                    ins = pe.matmul(ps_w[:, 0:QKV], xt1[:, k, :], wqkv[:, k, :], start=k == 0, stop=k == KC - 1)
                ins.then_inc(qkv_psum, 1)

            def stacked(parts, first):
                return parts[:, first:first + 2, :].rearrange("p h s -> p (h s)").bitcast(F32)

            def front_c(f, u):
                pe.wait_ge(qk_low, 2 * f + 2)
                if u:
                    pe.wait_ge(qt_ready, 2 * f + 1)
                elif not isinstance(f, int) or f >= 2:
                    pe.wait_ge(qtc_ready, 2 * (f - 1))
                for j in range(BLK):
                    first = 2 * BLK * u + 2 * j
                    ins = pe.transpose(ps_q[:, 128 * j:128 * j + 128], stacked(q_stk, first), ident[:, :])
                ins.then_inc(q_psum, 1)
                if u == 0:
                    for v in range(2):
                        ins = pe.transpose(ps_w[:, 128 * v:128 * v + 128], stacked(k_stk, 2 * v), ident[:, :])
                    ins.then_inc(k_psum, 1)

            def scores(kind, b, u):
                queries = qt if kind == SELF else qtc
                for g in (2 * u, 2 * u + 1):
                    pe.matmul(ps_s[g], ident_b[:, :], masks[:, kind, :], start=True, stop=False)
                for j in range(BLK):
                    for g in (2 * u, 2 * u + 1):
                        rows = slice(STK * (g % 2), STK * (g % 2) + STK)
                        keys = kt[rows, u, :] if kind == SELF else ktc[rows, u, j, :]
                        ins = pe.matmul(ps_s[g][:, 128 * j:128 * j + 128], queries[rows, u, j, :], keys,
                                        start=False, stop=j == BLK - 1)
                        if j == BLK - 1:
                            ins.then_inc(scores_psum[kind], 1)

            def transpose_probs(kind, b, u):
                for g in (2 * u, 2 * u + 1):
                    pe.wait_ge(probs_ready[kind], 4 * b + g + 1)
                    for j in range(BLK):
                        ins = pe.transpose(ps_s[g][:, 128 * j:128 * j + 128], probs[:, g, j, :], ident[:, :])
                    ins.then_inc(probs_t_psum[kind], 1)

            def values(kind, b, u):
                pe.wait_ge(probs_t_ready[kind][u], 2 * b + 2)
                pe.wait_ge(v_ready if kind == SELF else c_pad_ready, b + 1)
                for g in (2 * u, 2 * u + 1):
                    out_rows = slice(PAD * g, PAD * g + PAD)
                    if kind == SELF:
                        ins = pe.matmul(ps_o[out_rows, :], v_pad[:, g, :],
                                        probs_t[:, g, :, :].rearrange("p j n -> p (j n)"), start=True, stop=True)
                        continue
                    for j in range(BLK):
                        ins = pe.matmul(ps_o[out_rows, 128 * j:128 * j + 128], c_pad[:, j, g, :], probs_t[:, g, j, :],
                                        start=True, stop=True)
                ins.then_inc(values_psum[kind], 1)

            def turn_values(kind, b):
                pe.wait_ge(values_taken[kind], b + 1)
                for j in range(BLK):
                    ins = pe.transpose(ps_o[:, 128 * j:128 * j + 128], (values_t if kind == SELF else values_tc)[:, j, :],
                                       ident[:, :])
                ins.then_inc(rows_psum[kind], 1)

            def turn_attn(b):
                pe.wait_ge(attn_ready[SELF], b + 1)
                for k in range(KC):
                    ins = pe.transpose(ps_x[:, 128 * k:128 * k + 128], attn[:, 128 * k:128 * k + 128], ident[:, :])
                ins.then_inc(attn_t_psum, 1)

            def project(b):
                pe.wait_ge(attn_t_ready, b + 1)
                pe.wait_ge(kt_ready, b + 2)
                for k in range(KC):
                    ins = pe.matmul(ps_w[:, 0:D], attn_t[:, k, :], wo[:, k, :], start=k == 0, stop=k == KC - 1)
                ins.then_inc(wo_psum, 1)

            def cross_keys(c, u):
                pe.wait_ge(ctx_high, c + 1)
                pe.wait_ge(ctx_low, c + 1)
                if u:
                    pe.wait_ge(ktc_ready, 2 * c + 1)
                else:
                    pe.wait_ge(attn_t_ready, c + 1)
                for j in range(BLK):
                    first = BLK * j + 2 * u
                    ins = pe.transpose(ps_x[:, 128 * j:128 * j + 128], stacked(c_stk, first), ident[:, :])
                ins.then_inc(ct_psum, 1)

            def cross_queries(c, u):
                pe.wait_ge(xn2_low, c + 1)
                if u:
                    pe.wait_ge(qtc_ready, 2 * c + 1)
                else:
                    pe.wait_ge(qt_ready, 2 * (c + 2))
                for j in range(BLK):
                    first = BLK * j + 2 * u
                    ins = pe.transpose(ps_q[:, 128 * j:128 * j + 128], stacked(qc_stk, first), ident[:, :])
                ins.then_inc(qc_psum, 1)

            def third_norm(b, target):
                pe.wait_ge(xn3_ready, b + 1)
                for k in range(KC):
                    ins = pe.transpose(target[:, 128 * k:128 * k + 128], xn3[:, 128 * k:128 * k + 128], ident[:, :])
                ins.then_inc(xt3_psum, 1)

            def iteration(t, cross_on, tail_on):
                c = t - 1
                pe.wait_ge(qt_ready, 2 * t + 1)
                pe.wait_ge(kt_ready, t + 1)
                scores(SELF, t, 0)
                if tail_on:
                    turn_values(CROSS, t - 2)
                pe.wait_ge(qt_ready, 2 * t + 2)
                scores(SELF, t, 1)
                front_a(t + 1)
                if cross_on:
                    cross_keys(c, 0)
                    cross_queries(c, 0)
                transpose_probs(SELF, t, 0)
                front_b(t + 1)
                if cross_on:
                    cross_keys(c, 1)
                    cross_queries(c, 1)
                transpose_probs(SELF, t, 1)
                if cross_on:
                    pe.wait_ge(qtc_ready, 2 * t - 1)
                    pe.wait_ge(ktc_ready, 2 * t - 1)
                    pe.wait_ge(probs_t_ready[SELF][0], 2 * t + 2)
                    scores(CROSS, c, 0)
                if tail_on:
                    pe.wait_ge(attn_ready[CROSS], t - 1)
                values(SELF, t, 0)
                values(SELF, t, 1)
                if cross_on:
                    pe.wait_ge(qtc_ready, 2 * t)
                    pe.wait_ge(ktc_ready, 2 * t)
                if cross_on:
                    scores(CROSS, c, 1)
                if tail_on:
                    third_norm(t - 2, ps_x)
                turn_values(SELF, t)
                front_c(t + 1, 0)
                if cross_on:
                    transpose_probs(CROSS, c, 0)
                if tail_on:
                    pe.wait_ge(xtl_ready, t - 1)
                turn_attn(t)
                if cross_on:
                    transpose_probs(CROSS, c, 1)
                project(t)
                front_c(t + 1, 1)
                if cross_on:
                    values(CROSS, c, 0)
                    values(CROSS, c, 1)

            def three(outs, pairs_h, pairs_l, first, last):
                n = len(pairs_h)
                todo = [(pairs_h[k][0], pairs_h[k][1]) for k in range(n)]
                todo += [(pairs_h[k][0], pairs_l[k][1]) for k in range(n)]
                todo += [(pairs_l[k][0], pairs_h[k][1]) for k in range(n)]
                for i, (w, m) in enumerate(todo):
                    ins = pe.matmul(outs, w, m, start=first and i == 0, stop=last and i == len(todo) - 1,
                                    skip_group_check=not (first and last))
                return ins

            def route_logits(half):
                pe.wait_ge(gate_l_ready, 1)
                pe.wait_ge(xtl_ready, (half + 1) * HB)
                cols = slice(half * HALF, (half + 1) * HALF)
                three(ps_w[0:NCO + 1, :],
                      [(gate_h[:, k, :], xth[:, k, cols]) for k in range(KC)],
                      [(gate_l[:, k, :], xtl[:, k, cols]) for k in range(KC)], True, True).then_inc(lt_psum, 1)

            def turn_logits(half):
                pe.wait_ge(lt_ready, half + 1)
                for i in range(HB):
                    b = half * HB + i
                    ins = pe.transpose(ps_w[:, (NCO + 1) * i:(NCO + 1) * (i + 1)], logits_t[:, T * b:T * b + T],
                                       ident[0:NCO + 1, 0:NCO + 1])
                ins.then_inc(logits_psum, 1)

            def turn_coefs(half):
                pe.wait_ge(coef_ready, half + 1)
                for i in range(HB):
                    ins = pe.transpose(ps_w[0:PARTS * NCO, :].bitcast(BF16)[:, T * i:T * i + T],
                                       coef_b[:, half * HB + i, :, :].rearrange("p s e -> p (s e)"), ident_b[:, :])
                ins.then_inc(coef_psum, 1)

            def rows_of(n, k, half, early=False):
                cols = slice(half * HALF, (half + 1) * HALF)
                pe.wait_ge(wl_ready, n + 1)
                for part in range(2):
                    if not early:
                        pe.wait_ge([silu_ready, gu_ready][part], n - 1)
                    weights = [slice(256 * c + 128 * part, 256 * c + 128 * part + 128) for c in range(KC)]
                    three([ps_g, ps_u][part][k % 2][:, :],
                          [(w_h[:, k, weights[c]], xth[:, c, cols]) for c in range(KC)],
                          [(w_l[:, k, weights[c]], xtl[:, c, cols]) for c in range(KC)], True, True).then_inc(up_psum, 1)

            def keep_clock(n):
                for _ in range(n):
                    pe.matmul(ps_s[0], zero_b[:, 0:128], zero_b[:, :], start=True, stop=True)

            pe.wait_ge(zeros_ready, 1)
            keep_clock(WARM[0])
            pe.wait_ge(ident_loaded, 16)
            pe.wait_ge(pads_ready, 4)
            front_a(0)
            keep_clock(WARM[1])
            pe.wait_ge(wqkv_loaded, 16)
            front_b(0)
            keep_clock(WARM[2])
            front_c(0, 0)
            front_c(0, 1)
            keep_clock(WARM[3])
            pe.wait_ge(ident_b_ready, 1)
            pe.wait_ge(masks_loaded, 16)
            pe.wait_ge(wo_loaded, 32)
            iteration(0, False, False)
            pe.wait_ge(pads_ready, 10)
            iteration(1, True, False)
            with pe.Fori(2, B) as t:
                iteration(t, True, True)

            pe.wait_ge(x2_ready, B)
            route_logits(0)
            turn_values(CROSS, B - 2)
            cross_keys(B - 1, 0)
            cross_queries(B - 1, 0)
            turn_logits(0)
            cross_keys(B - 1, 1)
            cross_queries(B - 1, 1)
            scores(CROSS, B - 1, 0)
            pe.wait_ge(qtc_ready, 2 * B)
            pe.wait_ge(ktc_ready, 2 * B)
            third_norm(B - 2, ps_x)
            scores(CROSS, B - 1, 1)
            pe.wait_ge(xtl_ready, B - 1)
            rows_of(0, 0, 0, early=True)
            transpose_probs(CROSS, B - 1, 0)
            transpose_probs(CROSS, B - 1, 1)
            pe.wait_ge(attn_ready[CROSS], B - 1)
            values(CROSS, B - 1, 0)
            values(CROSS, B - 1, 1)

            def coefs_of(n, k, half):
                if not isinstance(n, int) or n:
                    pe.wait_ge(hid_ready, n)
                pe.matmul(ps_c[:, :], sel[:, k, :], coef_t[:, half * HALF:(half + 1) * HALF], start=True, stop=True
                          ).then_inc(co_psum, 1)

            def up(n, k, half):
                rows_of(n, k, half)
                coefs_of(n, k, half)

            def down(n, k, last=False):
                pe.wait_ge(hidl_ready, n + 1)
                for m in range(KC):
                    rows = slice(KC * 256 + 128 * m, KC * 256 + 128 * m + 128)
                    ins = three(ps_y[m][:, :], [(w_h[:, k, rows], hid_h[:, k % 2, :])],
                                [(w_l[:, k, rows], hid_l[:, k % 2, :])], False, last)
                ins.then_inc(down_done, 1)

            def open_rows():
                for m in range(KC):
                    pe.matmul(ps_y[m][:, :], zero_b[0:1, 0:128], zero_b[0:1, :], start=True, stop=False,
                              skip_group_check=True)

            def turn_rows(half, pair):
                m = 2 * half + pair
                pe.wait_ge(yt_ready, 2 * half + 2)
                if 0 < m < 3:
                    pe.wait_ge(y_ready, m)
                for i in range(2):
                    for k in range(KC):
                        at = T * (2 * pair + i)
                        ins = pe.transpose(rows_bank(m)[:, D * i + 128 * k:D * i + 128 * k + 128], y_t[:, k, at:at + T],
                                           ident[:, :])
                ins.then_inc(y_psum, 1)

            rows_of(1, 1, 0, early=True)
            turn_coefs(0)
            pe.wait_ge(coef_t_ready, 1)
            coefs_of(0, 0, 0)
            turn_values(CROSS, B - 1)
            rows_of(2, 2, 0)
            pe.wait_ge(attn_ready[CROSS], B)
            open_rows()
            coefs_of(1, 1, 0)
            down(0, 0)
            third_norm(B - 1, ps_w)
            rows_of(3, 3, 0)
            coefs_of(2, 2, 0)
            down(1, 1)
            route_logits(1)
            coefs_of(3, 3, 0)
            down(2, 2)
            rows_of(4, 0, 0)
            turn_logits(1)
            coefs_of(4, 0, 0)
            down(3, 3)
            for half in range(NHALF):
                if half:
                    for k in range(RING):
                        up(half * NC + k + 1, (k + 1) % RING, half)
                        if k == 0:
                            pe.wait_ge(yt_ready, 2 * half)
                            open_rows()
                        down(half * NC + k, k)
                        if k < 2:
                            turn_rows(half - 1, k)
                with pe.Fori(half * NC + RING, (half + 1) * NC - RING, RING) as n:
                    for k in range(RING):
                        up(n + k + 1, (k + 1) % RING, half)
                        down(n + k, k)
                for k in range(RING):
                    n = (half + 1) * NC - RING + k
                    if k < RING - 1:
                        up(n + 1, k + 1, half)
                    elif half + 1 < NHALF:
                        pe.wait_ge(coef_t_ready, 2)
                        up(n + 1, 0, half + 1)
                    if half == 0 and k == RING - 2:
                        turn_coefs(1)
                    down(n, k, last=k == RING - 1)
            for pair in range(2):
                turn_rows(NHALF - 1, pair)


def bf16_bits(table):
    return (table.astype(np.float32).view(np.uint32) >> 16).astype(np.uint16)


def lay_out(inputs):
    a = {k: np.asarray(v) for k, v in inputs.items()}
    f = np.float32
    got = {"x_in": a["x"], "ctx_in": a["ctx_2048"]}
    heads = np.arange(NH).reshape(2, 2, BLK).transpose(0, 2, 1).reshape(-1)
    columns = (heads[:, None] * DH + np.arange(DH)).reshape(-1)
    got["wqkv_in"] = np.concatenate([a["L0_attn_Wq"][:, columns], a["L0_attn_Wk"], a["L0_attn_Wv"]], axis=1)
    got["bqkv_in"] = np.concatenate([a["L0_attn_bq"][columns], a["L0_attn_bk"], a["L0_attn_bv"]])
    got["wo_in"] = a["L0_attn_Wo"]
    got["bo_in"] = a["L0_attn_bo"]
    half = DH // 2
    freq = (1.0 / f(10000.0) ** (np.arange(half, dtype=f) * f(2.0) / f(DH))).astype(f)
    angle = (np.arange(T, dtype=f)[:, None] * freq[None, :]).astype(f)
    cos, sin = np.cos(angle).astype(f), np.sin(angle).astype(f)
    heads = ROT // DH
    got["rope_in"] = np.stack([np.tile(np.concatenate([cos, cos], 1), (1, heads)),
                               np.tile(np.concatenate([-sin, sin], 1), (1, heads))], axis=1).astype(f)
    i, j = np.arange(T)[:, None], np.arange(T)[None, :]
    seen = [(i >= j) & ((j >= i - 64) | (j < 4)), i >= j]
    got["masks_in"] = np.stack([np.tile(np.where(s, 0.0, MASKED), (1, BLK)) for s in seen], axis=1)
    got["masks_in"] = bf16_bits(got["masks_in"])
    got["gate_in"] = np.concatenate([a["L0_ffn_gate_w"], a["L0_ffn_sgate_w"], np.zeros((1, D), f)]).T
    none = np.zeros((NC * 128 - HID, D), f)
    w13, shared = a["L0_ffn_w13"], a["L0_ffn_shared_gate_up_w"]
    g = np.concatenate([w13[:, :HE].reshape(-1, D), shared[:HS], none])
    u = np.concatenate([w13[:, HE:].reshape(-1, D), shared[HS:], none])
    d = np.concatenate([a["L0_ffn_w2"].transpose(0, 2, 1).reshape(-1, D), a["L0_ffn_shared_down_w"].T, none])
    gu = np.stack([g.reshape(NC, 128, KC, 128), u.reshape(NC, 128, KC, 128)], axis=1)
    gu = gu.transpose(0, 4, 3, 1, 2).reshape(NC, 128, KC * 256)
    got["chunks_in"] = np.concatenate([gu, d.reshape(NC, 128, D)], axis=2)
    owner = np.minimum(np.arange(NC * 128) // HE, NE)
    one = (owner.reshape(NC, 1, 128) == np.arange(NCO)[None, :, None])
    got["select_in"] = bf16_bits(np.tile(one, (1, PARTS, 1)))
    got["ident_in"] = np.eye(128, dtype=f)
    got["iota_in"] = np.arange(NE, dtype=f)
    return {k: np.ascontiguousarray(v) for k, v in got.items()}


def kernel(**inputs):
    import concourse.bacc as bacc
    from concourse.bass_utils import run_bass_kernel_spmd

    arrays = lay_out(inputs)
    nc = bacc.Bacc("TRN2", target_bir_lowering=False, num_devices=1)
    args = {k: nc.dram_tensor(f"{k}_dram", v.shape, mybir.dt.from_np(v.dtype), kind="ExternalInput").ap()
            for k, v in arrays.items()}
    out = nc.dram_tensor("out_dram", (B, T, D), F32, kind="ExternalOutput").ap()
    decoder_layer(nc, out=out, **args)
    r = run_bass_kernel_spmd(nc, [{f"{k}_dram": v for k, v in arrays.items()}], core_ids=[0])
    return r.results[0]["out_dram"]
```
